# Optimizing a Trainium2 kernel written in Bass

```python
import numpy as np
import jax
import jax.numpy as jnp

def _softmax(x, axis=-1):
    return jax.nn.softmax(x, axis=axis)

def _gelu(x):
    return jax.nn.gelu(x, approximate=True)

def _silu(x):
    return jax.nn.silu(x)

def _sigmoid(x):
    return jax.nn.sigmoid(x)

def _layernorm(x, axis=-1, eps=1e-05):
    m = jnp.mean(x, axis=axis, keepdims=True)
    v = jnp.var(x, axis=axis, keepdims=True)
    return (x - m) / jnp.sqrt(v + eps)

def _scatter_add(tgt, idx, src, axis=0):
    return tgt.at[idx].add(src)

def _segment_sum(src, seg, n):
    return jax.ops.segment_sum(src, seg, n)
kernel_name = 'mk_adj_ffn_d2_adj_r2_a02c66'

def setup_inputs(seed: int=0):
    np.random.seed(seed)
    _w = jnp.asarray

    def _rec_inputs():
        import jax
        import jax.numpy as jnp
        _gk = jax.random.key(seed)
        x = -0.0002928 + 1 * jax.random.normal(jax.random.fold_in(_gk, 1), (128, 64, 128), jnp.float32)
        _a = jax.random.bernoulli(jax.random.fold_in(_gk, 2), 0.125, (128, 64, 64))
        _a = jnp.logical_or(_a, jnp.swapaxes(_a, -1, -2))
        _a = jnp.logical_or(_a, jnp.eye(64, dtype=bool))
        _af = _a.astype(jnp.float32)
        _af = _af * jax.random.uniform(jax.random.fold_in(_gk, 3), (128, 64, 64), jnp.float32, 0.05, 1)
        adj = _af
        return (x, adj)
    x, adj = _rec_inputs()

    def _L0_gnn_setup():
        import jax, jax.numpy as jnp
        import numpy as np
        B, N, DIN, DOUT = (8, 1024, 128, 128)
        ALPHA = 0.2
        EPS = 1e-06
        key = jax.random.key(seed)
        k1, k2, k3, k4 = jax.random.split(key, 4)
        h = jax.random.normal(k1, (B, N, DIN), dtype=jnp.float32)
        adj = jax.random.uniform(k2, (B, N, N), dtype=jnp.float32)
        gain = 1.414
        limW = gain * np.sqrt(6.0 / (DIN + DOUT))
        W = jax.random.uniform(k3, (DIN, DOUT), minval=-limW, maxval=limW, dtype=jnp.float32)
        lima = gain * np.sqrt(6.0 / (2 * DOUT + 1))
        a = jax.random.uniform(k4, (2 * DOUT, 1), minval=-lima, maxval=lima, dtype=jnp.float32)
        return {'h': h, 'adj': adj, 'W': W, 'a': a}
    _L0_gnn_all = _L0_gnn_setup()
    _L0_gnn_in = {k: v for k, v in _L0_gnn_all.items() if k in ('W', 'a')}
    del _L0_gnn_all

    def _L0_ffn_setup():
        import jax, jax.numpy as jnp
        import numpy as np
        B, S, D, F, E, K = (8, 1024, 128, 512, 8, 2)
        key = jax.random.key(seed)
        ks = jax.random.split(key, 10)
        s = 0.02
        return {'x': jax.random.normal(ks[0], (B, S, D), dtype=jnp.float32), 'Wr': jax.random.normal(ks[1], (D, E), dtype=jnp.float32) * s, 'W1s': jax.random.normal(ks[2], (D, F), dtype=jnp.float32) * s, 'b1s': jnp.zeros((F,), dtype=jnp.float32), 'W2s': jax.random.normal(ks[3], (F, D), dtype=jnp.float32) * s, 'b2s': jnp.zeros((D,), dtype=jnp.float32), 'W1p': jax.random.normal(ks[4], (E, D, F), dtype=jnp.float32) * s, 'b1p': jnp.zeros((E, F), dtype=jnp.float32), 'W2p': jax.random.normal(ks[5], (E, F, D), dtype=jnp.float32) * s, 'b2p': jnp.zeros((E, D), dtype=jnp.float32)}
    _L0_ffn_all = _L0_ffn_setup()
    _L0_ffn_in = {k: v for k, v in _L0_ffn_all.items() if k in ('Wr', 'W1s', 'b1s', 'W2s', 'b2s', 'W1p', 'b1p', 'W2p', 'b2p')}
    del _L0_ffn_all

    def _L1_gnn_setup():
        import jax, jax.numpy as jnp
        import numpy as np
        B, N, D = (4, 2048, 128)
        DENSITY = 0.02
        key = jax.random.key(seed)
        kx, ka1, ka2, kwt, kbt, kwh, kth = jax.random.split(key, 7)
        x = jax.random.normal(kx, (B, N, D), dtype=jnp.float32)
        mask = jax.random.uniform(ka1, (B, N, N)) < DENSITY
        vals = jax.random.uniform(ka2, (B, N, N), dtype=jnp.float32)
        adj = jnp.where(mask, vals, 0.0).astype(jnp.float32)
        s = 0.02
        W_t = s * jax.random.normal(kwt, (D, D), dtype=jnp.float32)
        b_t = s * jax.random.normal(kbt, (D,), dtype=jnp.float32)
        W_h = s * jax.random.normal(kwh, (D, D), dtype=jnp.float32)
        theta = s * jax.random.normal(kth, (D, D), dtype=jnp.float32)
        return {'x': x, 'adj': adj, 'W_t': W_t, 'b_t': b_t, 'W_h': W_h, 'theta': theta}
    _L1_gnn_all = _L1_gnn_setup()
    _L1_gnn_in = {k: v for k, v in _L1_gnn_all.items() if k in ('W_t', 'b_t', 'W_h', 'theta')}
    del _L1_gnn_all

    def _L1_ffn_setup():
        import jax, jax.numpy as jnp
        import numpy as np
        B, S, D, E, H, K = (4, 2048, 128, 8, 256, 2)
        key = jax.random.key(seed)
        ks = jax.random.split(key, 6)
        x = jax.random.normal(ks[0], (B, S, D), jnp.float32)
        Wg = jax.random.normal(ks[1], (D, E), jnp.float32) * 0.02
        bg = jnp.zeros((E,), jnp.float32)
        W1 = jax.random.normal(ks[2], (E, D, H), jnp.float32) * 0.02
        b1 = jnp.zeros((E, H), jnp.float32)
        W2 = jax.random.normal(ks[3], (E, H, D), jnp.float32) * 0.02
        b2 = jnp.zeros((E, D), jnp.float32)
        return {'x': x, 'Wg': Wg, 'bg': bg, 'W1': W1, 'b1': b1, 'W2': W2, 'b2': b2}
    _L1_ffn_all = _L1_ffn_setup()
    _L1_ffn_in = {k: v for k, v in _L1_ffn_all.items() if k in ('Wg', 'bg', 'W1', 'b1', 'W2', 'b2')}
    del _L1_ffn_all
    return {'x': x, 'adj': adj, 'L0_gnn_W': _L0_gnn_in['W'], 'L0_gnn_a': _L0_gnn_in['a'], 'L0_ffn_Wr': _L0_ffn_in['Wr'], 'L0_ffn_W1s': _L0_ffn_in['W1s'], 'L0_ffn_b1s': _L0_ffn_in['b1s'], 'L0_ffn_W2s': _L0_ffn_in['W2s'], 'L0_ffn_b2s': _L0_ffn_in['b2s'], 'L0_ffn_W1p': _L0_ffn_in['W1p'], 'L0_ffn_b1p': _L0_ffn_in['b1p'], 'L0_ffn_W2p': _L0_ffn_in['W2p'], 'L0_ffn_b2p': _L0_ffn_in['b2p'], 'L1_gnn_W_t': _L1_gnn_in['W_t'], 'L1_gnn_b_t': _L1_gnn_in['b_t'], 'L1_gnn_W_h': _L1_gnn_in['W_h'], 'L1_gnn_theta': _L1_gnn_in['theta'], 'L1_ffn_Wg': _L1_ffn_in['Wg'], 'L1_ffn_bg': _L1_ffn_in['bg'], 'L1_ffn_W1': _L1_ffn_in['W1'], 'L1_ffn_b1': _L1_ffn_in['b1'], 'L1_ffn_W2': _L1_ffn_in['W2'], 'L1_ffn_b2': _L1_ffn_in['b2']}

def reference(x, adj, L0_gnn_W, L0_gnn_a, L0_ffn_Wr, L0_ffn_W1s, L0_ffn_b1s, L0_ffn_W2s, L0_ffn_b2s, L0_ffn_W1p, L0_ffn_b1p, L0_ffn_W2p, L0_ffn_b2p, L1_gnn_W_t, L1_gnn_b_t, L1_gnn_W_h, L1_gnn_theta, L1_ffn_Wg, L1_ffn_bg, L1_ffn_W1, L1_ffn_b1, L1_ffn_W2, L1_ffn_b2):
    import jax
    import jax.numpy as jnp

    def _L0_gnn_ref(h, adj, W, a):
        import jax, jax.numpy as jnp
        import numpy as np
        B, N, DIN, DOUT = (8, 1024, 128, 128)
        ALPHA = 0.2
        EPS = 1e-06
        Wh = jnp.einsum('bnd,df->bnf', h, W)
        a1 = a[:DOUT, 0]
        a2 = a[DOUT:, 0]
        s1 = Wh @ a1
        s2 = Wh @ a2
        e = s1[:, :, None] + s2[:, None, :]
        e = jnp.where(e > 0, e, ALPHA * e)
        e = e + jnp.log(adj + EPS)
        alpha_w = jax.nn.softmax(e, axis=-1)
        h_prime = jnp.einsum('bij,bjf->bif', alpha_w, Wh)
        return h_prime

    def _L0_ffn_ref(x, Wr, W1s, b1s, W2s, b2s, W1p, b1p, W2p, b2p):
        import jax, jax.numpy as jnp
        import numpy as np
        B, S, D, F, E, K = (8, 1024, 128, 512, 8, 2)
        gelu = lambda t: jax.nn.gelu(t, approximate=False)
        shared = gelu(x @ W1s + b1s) @ W2s + b2s
        rw = jax.nn.softmax(x @ Wr, axis=-1)
        topw, topi = jax.lax.top_k(rw, K)
        topw = topw / jnp.sum(topw, axis=-1, keepdims=True)
        mask = jnp.sum(jax.nn.one_hot(topi, E, dtype=topw.dtype) * topw[..., None], axis=-2)
        h = gelu(jnp.einsum('bsd,edf->bsef', x, W1p) + b1p)
        priv = jnp.einsum('bsef,efd->bsed', h, W2p) + b2p
        routed = jnp.einsum('bsed,bse->bsd', priv, mask)
        return shared + routed

    def _L1_gnn_ref(x, adj, W_t, b_t, W_h, theta):
        import jax, jax.numpy as jnp
        import numpy as np
        B, N, D = (4, 2048, 128)
        DENSITY = 0.02
        in_degrees = jnp.sum(adj, axis=-1)
        norm = jnp.power(in_degrees + 1e-06, -0.5)[..., None]
        f_hom = jnp.einsum('bnd,de->bne', x, theta) * norm
        f_hom = jnp.einsum('bnm,bmd->bnd', adj, f_hom) * norm
        f_het = jnp.einsum('bnd,de->bne', x, W_h)
        gate = jax.nn.sigmoid(jnp.einsum('bnd,de->bne', x, W_t) + b_t)
        out = gate * f_hom + (1.0 - gate) * f_het
        return jax.nn.elu(out)

    def _L1_ffn_ref(x, Wg, bg, W1, b1, W2, b2):
        import jax, jax.numpy as jnp
        import numpy as np
        B, S, D, E, H, K = (4, 2048, 128, 8, 256, 2)
        Bv, Sv, Dv = x.shape
        gate_scores = x @ Wg + bg
        _, idx = jax.lax.top_k(gate_scores, K)
        mask = jax.nn.one_hot(idx, E, dtype=x.dtype).sum(axis=-2)
        xf = x.reshape(-1, Dv)
        mf = mask.reshape(-1, E)
        h = jax.nn.gelu(jnp.einsum('td,edh->teh', xf, W1) + b1[None], approximate=False)
        y = jnp.einsum('teh,ehd->ted', h, W2) + b2[None]
        out = jnp.einsum('ted,te->td', y, mf)
        return out.reshape(Bv, Sv, Dv)
    x = x + _L0_gnn_ref(_layernorm(x, axis=-1), adj, L0_gnn_W, L0_gnn_a)
    x = x + _L0_ffn_ref(_layernorm(x, axis=-1), L0_ffn_Wr, L0_ffn_W1s, L0_ffn_b1s, L0_ffn_W2s, L0_ffn_b2s, L0_ffn_W1p, L0_ffn_b1p, L0_ffn_W2p, L0_ffn_b2p)
    x = x + _L1_gnn_ref(_layernorm(x, axis=-1), adj, L1_gnn_W_t, L1_gnn_b_t, L1_gnn_W_h, L1_gnn_theta)
    x = x + _L1_ffn_ref(_layernorm(x, axis=-1), L1_ffn_Wg, L1_ffn_bg, L1_ffn_W1, L1_ffn_b1, L1_ffn_W2, L1_ffn_b2)
    return x

_drawn_inputs = setup_inputs


def setup_inputs(seed=0):
    import zlib

    import numpy as np

    out = dict(_drawn_inputs(seed))
    spreads = {'L0_ffn_b1s': (0.0, 0.283),
     'L0_ffn_b2s': (0.0, 0.1),
     'L0_ffn_b1p': (0.0, 0.389),
     'L0_ffn_b2p': (0.0, 0.1),
     'L1_ffn_bg': (0.0, 0.1),
     'L1_ffn_b1': (0.0, 0.402),
     'L1_ffn_b2': (0.0, 0.1)}
    factors = {'L1_gnn_W_t': 3.769, 'L1_gnn_b_t': 38.261}
    for name, (base, spread) in spreads.items():
        noise = np.random.default_rng([zlib.crc32(name.encode()), seed]).standard_normal(out[name].shape)
        drawn = base * np.exp(spread * noise) if base else spread * noise
        out[name] = jnp.asarray(drawn.astype(out[name].dtype))
    for name, factor in factors.items():
        out[name] = (out[name] * factor).astype(out[name].dtype)
    return out
```

```python
from contextlib import ExitStack

import concourse.bass as bass
from concourse import mybir

F32 = mybir.dt.float32
F16 = mybir.dt.float16
ALU = mybir.AluOpType
ACT = mybir.ActivationFunctionType
AX_X = mybir.AxisListType.X

P = 128
D = 128
C = 4
BLK = C * P
E = 8
TOPS = 2
WSCALE = 256.0
ALPHA = 0.2
NOT_AGAIN = -1.0e30

H_SLOTS = 4
LAG = 3


def mk_adj_ffn_kernel(
    nc, x, adj, gat_W, gat_a, Wr, W1s, b1s, W2s, b2s, W1p, b1p, W2p, b2p,
    W_t, b_t, W_h, theta, Wg, bg, W1, b1, W2, b2, out,
):
    graphs, nodes, _ = x.shape
    gpt = P // nodes
    NB = graphs * nodes // BLK
    SH = W1s.shape[1] // P
    K0 = W1p.shape[2] // P
    K1 = W1.shape[2] // P
    A_SLOTS = SH + E * K0
    SLOTS = A_SLOTS + E * K1
    UNIT_LEN = [SH] + [K0] * E + [K1] * E
    UNITS = len(UNIT_LEN)
    A_UNITS = 1 + E
    UNIT_OF = [u for u, k in enumerate(UNIT_LEN) for _ in range(k)]
    FIRST = [sum(UNIT_LEN[:u]) for u in range(UNITS)]
    LAST = [sum(UNIT_LEN[:u + 1]) - 1 for u in range(UNITS)]
    assert gpt == 2 and A_SLOTS % H_SLOTS == 0 and SLOTS % H_SLOTS == 0 and SH == K0

    def count(i, per_block, db, n):
        return per_block * i + (per_block * db + n)

    def chunks(i, s):
        if isinstance(i, int) and i == 0:
            return s
        if isinstance(i, int) and i == NB:
            return A_SLOTS + SLOTS * (NB - 1) + s - A_SLOTS
        return SLOTS * i + (A_SLOTS - SLOTS + s)

    def units(i, u):
        if isinstance(i, int) and i == 0:
            return u
        if isinstance(i, int) and i == NB:
            return A_UNITS + UNITS * (NB - 1) + u - A_UNITS
        return UNITS * i + (A_UNITS - UNITS + u)

    def sums(i, u):
        n = max(u - 1, 0) - (1 if u > A_UNITS else 0)
        if isinstance(i, int) and i == 0:
            return n
        if isinstance(i, int) and i == NB:
            return E + (2 * E - 1) * (NB - 1) + n - E
        return (2 * E - 1) * i + (E - (2 * E - 1) + n)

    def need(eng, sem, value):
        if not isinstance(value, int) or value > 0:
            eng.wait_ge(sem, value)

    def in_blocks(eng, body):
        body(-1)
        body(0)
        body(1)
        with eng.Fori(2, NB - 1) as i:
            body(i)
        body(NB - 1)
        body(NB)

    def has(i):
        if not isinstance(i, int):
            return True, True, True
        return 0 <= i < NB, 1 <= i <= NB, i + 1 < NB

    x_v = x.rearrange("(b c g) n d -> b (g n) c d", c=C, g=gpt)
    out_v = out.rearrange("(b c g) n d -> b (g n) c d", c=C, g=gpt)
    adj_v = adj.rearrange("(b c g) n m -> b (g n) c m", c=C, g=gpt)

    def block_of(view, b):
        return view[b] if isinstance(b, int) else view[bass.ds(b, 1)].rearrange("b p c d -> (b p) c d")

    with ExitStack() as ctx:
        def sb(name, shape, dt=F32):
            return ctx.enter_context(nc.sbuf_tensor(name, shape, dt))

        def sem(name):
            return ctx.enter_context(nc.semaphore(name))

        ps_h = [ctx.enter_context(nc.psum_tensor(f"ps_h{k}", [P, BLK], F32)) for k in range(2)]
        ps_y = [ctx.enter_context(nc.psum_tensor(f"ps_y{k}", [P, BLK], F32)) for k in range(2)]
        s0, s1, s2, s3 = (ctx.enter_context(nc.psum_tensor(f"ps_s{k}", [P, BLK], F32)) for k in range(4))

        w1h = sb("w1h", [P, SLOTS, P], F16)
        w1l = sb("w1l", [P, SLOTS, P], F16)
        w2h = sb("w2h", [P, SLOTS, P], F16)
        w2l = sb("w2l", [P, SLOTS, P], F16)
        PIECES = SLOTS // C
        STAGES = 8
        stage = [sb(f"stage{k}", [P, C, P]) for k in range(STAGES)]
        gat_w = sb("gat_w", [P, D])
        theta_w = sb("theta_w", [P, D])
        wh_w = sb("wh_w", [P, D])
        wt_w = sb("wt_w", [P, D])
        gate_f = sb("gate_f", [P, 2, E])
        gate_h = sb("gate_h", [P, 2, E], F16)
        gate_l = sb("gate_l", [P, 2, E], F16)
        ROWS = SLOTS + UNITS + 3
        A_ROW = SLOTS + UNITS
        rows = sb("rows", [ROWS, P])
        cols = sb("cols", [P, ROWS])
        b2x = sb("b2x", [P, UNITS])
        bt_half = sb("bt_half", [P, 1])
        gat_wT = sb("gat_wT", [P, D])
        wa = sb("wa", [P, 2])
        wa2_rep = sb("wa2_rep", [P, P])
        bg_b = sb("bg_b", [P, E])
        ident = sb("ident", [P, P])
        ones = sb("ones", [P, P])
        ramp = sb("ramp", [P, E])
        neg_half = sb("neg_half", [P, C])
        carrier = sb("carrier", [P, 1])
        eps = sb("eps", [P, 2, C])

        x_in = sb("x_in", [P, C, D])
        adj_a = sb("adj_a", [P, C, nodes])
        st_a = sb("st_a", [P, C, 6])
        mv_a = sb("mv_a", [P, C, 2])
        rs_a = sb("rs_a", [P, 2, C])
        xn_a = sb("xn_a", [P, C, D])
        xt_a = sb("xt_a", [P, BLK])
        s1c = sb("s1c", [P, 4, C])
        u_a = sb("u_a", [P, C, nodes])
        e_a = sb("e_a", [P, C, nodes])
        pr_a = sb("pr_a", [P, C, P])
        pt_a = sb("pt_a", [P, BLK])
        wh_a = sb("wh_a", [P, BLK])
        rr_a = sb("rr_a", [P, C])
        x1n = sb("x1n", [P, C, D])
        x1 = sb("x1", [P, C, D])
        adj_b = sb("adj_b", [P, C, nodes])
        st_b = sb("st_b", [P, C, 6])
        mv_b = sb("mv_b", [P, C, 2])
        rs_b = sb("rs_b", [P, 2, C])
        dg_b = sb("dg_b", [P, 3, C])
        an_b = sb("an_b", [P, C, P])
        at_b = sb("at_b", [P, BLK])
        xn_b = sb("xn_b", [P, C, D])
        xt_b = sb("xt_b", [P, BLK])
        f_b = sb("f_b", [P, C, D])
        tg_b = sb("tg_b", [P, BLK])
        het_b = sb("het_b", [P, BLK])
        d_b = sb("d_b", [P, BLK])
        o_b = sb("o_b", [P, BLK])
        x2 = sb("x2", [P, C, D])
        x3 = sb("x3", [P, C, D])
        x4 = sb("x4", [P, C, D])

        class Gate:
            def __init__(self, n):
                self.st = sb(f"st_f{n}", [P, C, 6])
                self.mv = sb(f"mv_f{n}", [P, C, 2])
                self.rs = sb(f"rs_f{n}", [P, 2, C])
                self.xn = sb(f"xn_f{n}", [P, C, D])
                self.hi = sb(f"xt_hi{n}", [P, BLK], F16)
                self.lo = sb(f"xt_lo{n}", [P, BLK], F16)
                self.lg = sb(f"lg{n}", [P, C, E])
                self.lg2 = sb(f"lg2{n}", [P, C, E])
                self.q = sb(f"q{n}", [P, 4, C, E])
                self.one = sb(f"one{n}", [P, 2, C, E])
                self.m = sb(f"m{n}", [P, 5, C])
                self.th = sb(f"th{n}", [P, C])
                self.w = sb(f"w{n}", [P, 2, C])
                self.mask = sb(f"mask{n}", [P, E, C])
                self.mt = sb(f"mt{n}", [E * C, P])
                self.mb = sb(f"mb{n}", [P, E, BLK])
                self.dram = nc.dram_tensor(f"mask_rows{n}", (E * C, P), F32, kind="Internal").ap()
                self.acc = sb(f"acc{n}", [P, BLK])
                self.stats, self.rstd, self.xn_s, self.tr, self.hi_s, self.lo_s, self.logits = (
                    sem(f"{s}{n}") for s in ("stats", "rstd", "xn", "tr", "hi", "lo", "logits"))
                self.top, self.tanh, self.mask_d, self.mask_tr, self.mask_row, self.acc_tr = (
                    sem(f"{s}{n}") for s in ("top", "tanh", "mask_d", "mask_tr", "mask_row", "acc_tr"))
                self.row_out = sem(f"mask_out{n}")
                self.mb_in = [sem(f"mask_in{n}_{k}") for k in range(E // 2)]

        gates = [Gate(0), Gate(1)]
        scaled = sb("scaled", [P, BLK])
        h32 = [sb(f"h32_{k}", [P, BLK]) for k in range(H_SLOTS)]
        hhi = [sb(f"hhi_{k}", [P, BLK], F16) for k in range(H_SLOTS)]
        hlo = [sb(f"hlo_{k}", [P, BLK], F16) for k in range(H_SLOTS)]

        small_in = sem("small_in")
        stage_in = [sem(f"stage_in{k}") for k in range(STAGES)]
        w_hi = sem("w_hi")
        w_lo = sem("w_lo")
        consts = sem("consts")
        zeroed = sem("zeroed")
        setup_pe = sem("setup_pe")
        setup_dve = sem("setup_dve")
        gate_hi = sem("gate_hi")

        x_landed, adja_landed, adjb_landed, stored = sem("x_landed"), sem("adja_landed"), sem("adjb_landed"), sem("stored")
        a_stats, a_rstd, a_xn, a_tr, a_xt = (sem(n) for n in ("a_stats", "a_rstd", "a_xn", "a_tr", "a_xt"))
        a_s, a_soft, a_exp, a_prob, a_ptr, a_pt, a_wh, a_whs, a_out, a_x1n, x1_made = (sem(n) for n in (
            "a_s", "a_soft", "a_exp", "a_prob", "a_ptr", "a_pt", "a_wh", "a_whs", "a_out", "a_x1n", "x1_made"))
        b_stats, b_rstd, b_xn, b_tr, b_xt, b_deg, b_norm, b_adjn = (sem(n) for n in (
            "b_stats", "b_rstd", "b_xn", "b_tr", "b_xt", "b_deg", "b_norm", "b_adjn"))
        b_f, b_fn, b_atr, b_at, b_gate, b_tanh, b_het, b_hets, b_hom, b_mix, b_exp, b_elu, b_otr, x3_made = (
            sem(n) for n in ("b_f", "b_fn", "b_atr", "b_at", "b_gate", "b_tanh", "b_het", "b_hets", "b_hom",
                             "b_mix", "b_exp", "b_elu", "b_otr", "x3_made"))
        x2_made, x4_made = sem("x2_made"), sem("x4_made")
        up = sem("up")
        gelu = sem("gelu")
        low = sem("low")
        down = sem("down")
        evac = sem("evac")
        summed = sem("summed")
        SMALL = 15
        CONSTS = 7 + E

        STATS, SOFT, TOP, X1N, MIX = 2 * C, 8, 13, C + 1, 4

        def bcast(ap, n):
            return ap.unsqueeze(2).to_broadcast([ap.shape[0], ap.shape[1], n])

        block = ctx.enter_context(nc.Block())

        @block.sync
        def _(sp):
            for dst, src in (
                (gat_w[:], gat_W), (theta_w[:], theta), (wh_w[:], W_h), (wt_w[:], W_t),
                (gate_f[:, 0], Wr), (gate_f[:, 1], Wg),
                (rows[0:SH], b1s.rearrange("(k p) -> k p", p=P)),
                (rows[SH:A_SLOTS], b1p.rearrange("e (k p) -> (e k) p", p=P)),
                (rows[A_SLOTS:SLOTS], b1.rearrange("e (k p) -> (e k) p", p=P)),
                (rows[SLOTS:SLOTS + 1], b2s.rearrange("(k p) -> k p", p=P)),
                (rows[SLOTS + 1:SLOTS + 1 + E], b2p), (rows[SLOTS + 1 + E:SLOTS + UNITS], b2),
                (rows[A_ROW:A_ROW + 2], gat_a.rearrange("(k p) u -> k (p u)", p=P)),
                (rows[A_ROW + 2:A_ROW + 3], b_t.rearrange("(k p) -> k p", p=P)),
                (bg_b[:], bg.rearrange("(u e) -> u e", u=1).to_broadcast([P, E])),
            ):
                sp.dma_start(dst, src).then_inc(small_in, 16)

            def weight_pieces():
                for n in range(2 * PIECES):
                    p, second = n // 2, n % 2
                    if n >= STAGES:
                        sp.wait_ge(w_lo, n - STAGES + 1)
                    if p == 0:
                        src = W2s.rearrange("(k p) d -> p k d", p=P) if second else W1s.rearrange("d (k p) -> d k p", p=P)
                        sp.dma_start(stage[n % STAGES][:], src).then_inc(stage_in[n % STAGES], 16)
                    elif p <= E:
                        src = (W2p[p - 1].rearrange("(k p) d -> p k d", p=P) if second
                               else W1p[p - 1].rearrange("d (k p) -> d k p", p=P))
                        sp.dma_start(stage[n % STAGES][:], src).then_inc(stage_in[n % STAGES], 16)
                    else:
                        e = (p - 1 - E) * (C // K1)
                        for j in range(C // K1):
                            src = (W2[e + j].rearrange("(k p) d -> p k d", p=P) if second
                                   else W1[e + j].rearrange("d (k p) -> d k p", p=P))
                            sp.dma_start(stage[n % STAGES][:, j * K1:(j + 1) * K1], src)\
                              .then_inc(stage_in[n % STAGES], 16)

            def masks_out(i, db, g):
                sp.wait_ge(g.mask_row, count(i, 1, db, 1))
                sp.dma_start(g.dram, g.mt[:]).then_inc(g.row_out, 16)
                sp.wait_ge(g.row_out, count(i, 16, db, 16))
                for k in range(E // 2):
                    src = g.dram[2 * k * C:2 * (k + 1) * C].rearrange("(u r) p -> u (r p)", u=1)
                    sp.dma_start(g.mb[:, 2 * k:2 * k + 2, :].rearrange("p e t -> p (e t)"),
                                 src.to_broadcast([P, 2 * BLK])).then_inc(g.mb_in[k], 16)

            def iteration(i):
                experts0, layer1, next0 = has(i)
                if next0:
                    src_x, src_a = block_of(x_v, i + 1), block_of(adj_v, i + 1)
                    need(sp, a_x1n, count(i, X1N, 1, 0))
                    sp.dma_start(x_in[:], src_x).then_inc(x_landed, 16)
                    sp.dma_start(adj_a[:], src_a).then_inc(adja_landed, 16)
                if layer1:
                    src_b = block_of(adj_v, i - 1)
                    need(sp, b_adjn, count(i, 2, -1, 0))
                    sp.dma_start(adj_b[:], src_b).then_inc(adjb_landed, 16)
                if isinstance(i, int) and i == -1:
                    weight_pieces()
                if layer1:
                    masks_out(i, -1, gates[1])
                if next0:
                    masks_out(i, 1, gates[0])
                if layer1:
                    dst = block_of(out_v, i - 1)
                    sp.wait_ge(x4_made, count(i, 1, -1, 1))
                    sp.dma_start(dst, x4[:]).then_inc(stored, 16)

            in_blocks(sp, iteration)
            sp.wait_ge(stored, 16 * NB)

        @block.gpsimd
        def _(pool):
            pool.memset(ident[:], 0.0).then_inc(consts, 1)
            pool.memset(ones[:], 1.0).then_inc(consts, 1)
            pool.memset(neg_half[:], -0.5).then_inc(consts, 1)
            pool.memset(eps[:, 0, :], 1.0e-5).then_inc(consts, 1)
            pool.memset(eps[:, 1, :], 1.0e-6).then_inc(consts, 1)
            for e in range(E):
                pool.memset(ramp[:, e:e + 1], float(E - e)).then_inc(consts, 1)
            pool.memset(an_b[:], 0.0).then_inc(consts, 1)
            pool.wait_ge(consts, 1)
            pool.affine_select(out=ident[:], in_=ident[:], compare_op=ALU.not_equal, fill=1.0,
                               base=0, pattern=[[-1, P]], channel_multiplier=1).then_inc(consts, 1)
            pool.wait_ge(consts, CONSTS)

            def rstd(i, db, mv, rs, stats, done):
                pool.wait_ge(stats, count(i, STATS, db, STATS))
                pool.tensor_tensor(rs[:, 0, :], mv[:, :, 1], eps[:, 0, :], ALU.add).then_inc(done, 1)
                pool.wait_ge(done, count(i, 2, db, 1))
                pool.tensor_tensor(rs[:, 1, :], rs[:, 0, :], neg_half[:], ALU.pow).then_inc(done, 1)

            def adj_norm(i, db):
                pool.wait_ge(b_deg, count(i, 1, db, 1))
                pool.tensor_tensor(dg_b[:, 1, :], dg_b[:, 0, :], eps[:, 1, :], ALU.add).then_inc(b_norm, 1)
                pool.wait_ge(b_norm, count(i, 2, db, 1))
                pool.tensor_tensor(dg_b[:, 2, :], dg_b[:, 1, :], neg_half[:], ALU.pow).then_inc(b_norm, 1)
                pool.wait_ge(b_norm, count(i, 2, db, 2))
                need(pool, b_at, count(i, 1, db, 0))
                for h in range(gpt):
                    ps = slice(h * nodes, (h + 1) * nodes)
                    pool.tensor_tensor(an_b[ps, :, ps], adj_b[ps, :, :], bcast(dg_b[ps, 2, :], nodes),
                                       ALU.mult).then_inc(b_adjn, 1)
                    pool.wait_ge(b_adjn, count(i, 2, db, h + 1))

            def iteration(i):
                experts0, layer1, next0 = has(i)
                if layer1:
                    rstd(i, -1, mv_b, rs_b, b_stats, b_rstd)
                    adj_norm(i, -1)
                if next0:
                    rstd(i, 1, mv_a, rs_a, a_stats, a_rstd)
                if layer1:
                    rstd(i, -1, gates[1].mv, gates[1].rs, gates[1].stats, gates[1].rstd)
                if next0:
                    rstd(i, 1, gates[0].mv, gates[0].rs, gates[0].stats, gates[0].rstd)

            in_blocks(pool, iteration)

        @block.scalar
        def _(act):
            def weight_piece(n):
                p = n // 2
                hi = (w2h if n % 2 else w1h)[:, C * p:C * p + C, :]
                halves = 1 if p <= E else C // K1
                before = sum(16 * (1 if m // 2 <= E else C // K1) for m in range(n % STAGES, n, STAGES))
                act.wait_ge(stage_in[n % STAGES], before + 16 * halves)
                act.activation(hi, stage[n % STAGES][:], ACT.Copy, scale=WSCALE).then_inc(w_hi, 1)

            def setup():
                act.wait_ge(small_in, 16 * SMALL)
                act.activation(gate_h[:], gate_f[:], ACT.Copy, scale=WSCALE).then_inc(gate_hi, 1)

            def copy_out(i, db, dst, src, ready, done, free=None):
                act.wait_ge(ready, count(i, 1, db, 1))
                if free is not None:
                    need(act, *free)
                act.activation(dst, src, ACT.Copy).then_inc(done, 1)

            def gate_tanh(i, db, g):
                act.wait_ge(g.top, count(i, TOP, db, TOP))
                act.activation(g.th[:], g.m[:, 4, :], ACT.Tanh, scale=0.5).then_inc(g.tanh, 1)

            def mask_rows(i, db, g, units_before):
                need(act, evac, units_before)
                act.wait_ge(g.mask_tr, count(i, 1, db, 1))
                need(act, g.row_out, count(i, 16, db, 0))
                act.activation(g.mt[:], (s1 if g is gates[0] else s3)[0:E * C, 0:P], ACT.Copy,
                               scale=1.0 / WSCALE).then_inc(g.mask_row, 1)

            def iteration(i):
                experts0, layer1, next0 = has(i)
                for s in range(SLOTS):
                    if next0:
                        if s == 8:
                            copy_out(i, 1, xt_a[:], s0[:], a_tr, a_xt)
                        if s == 14:
                            copy_out(i, 1, wh_a[:], s1[:], a_wh, a_whs)
                        if s == 15:
                            act.wait_ge(a_soft, count(i, SOFT, 1, SOFT))
                            act.activation(e_a[:], u_a[:], ACT.Exp).then_inc(a_exp, 1)
                        if s == 20:
                            copy_out(i, 1, pt_a[:], s0[:], a_ptr, a_pt)
                        if s == 37:
                            if experts0:
                                act.wait_ge(up, chunks(i, A_SLOTS))
                            copy_out(i, 1, gates[0].hi[:], s0[:], gates[0].tr, gates[0].hi_s)
                        if s == 42:
                            gate_tanh(i, 1, gates[0])
                        if s == 46:
                            mask_rows(i, 1, gates[0], units(i, A_UNITS) if experts0 else 0)
                    if layer1:
                        if s == 5:
                            copy_out(i, -1, xt_b[:], s2[:], b_tr, b_xt)
                        if s == 9:
                            copy_out(i, -1, at_b[:], s2[:], b_atr, b_at)
                        if s == 10:
                            act.wait_ge(b_gate, count(i, 1, -1, 1))
                            act.activation(tg_b[:], s3[:], ACT.Tanh, bias=bt_half[:, 0:1], scale=0.5)\
                               .then_inc(b_tanh, 1)
                        if s == 12:
                            copy_out(i, -1, het_b[:], s2[:], b_het, b_hets)
                        if s == 15:
                            act.wait_ge(b_mix, count(i, MIX, -1, MIX))
                            act.activation(d_b[:], d_b[:], ACT.Exp).then_inc(b_exp, 1)
                        if s == 24:
                            copy_out(i, -1, gates[1].hi[:], s2[:], gates[1].tr, gates[1].hi_s)
                        if s == 31:
                            mask_rows(i, -1, gates[1], units(i, 0) if experts0 else units(i, A_UNITS))
                    if (experts0 and s < A_SLOTS) or (layer1 and s >= A_SLOTS):
                        k = s % H_SLOTS
                        act.wait_ge(up, chunks(i, s + 1))
                        need(act, down, chunks(i, s + 1) - H_SLOTS)
                        act.activation(h32[k][:], ps_h[s % 2][:], ACT.Gelu, bias=cols[:, s:s + 1],
                                       scale=1.0 / WSCALE).then_inc(gelu, 1)
                        act.activation(hhi[k][:], ps_h[s % 2][:], ACT.Gelu, bias=cols[:, s:s + 1],
                                       scale=1.0 / WSCALE).then_inc(gelu, 1)
                    if isinstance(i, int) and i == -1 and s < 2 * PIECES:
                        if s == 0:
                            setup()
                        weight_piece(s)

            in_blocks(act, iteration)

        @block.vector
        def _(dve):
            def weight_piece(n):
                p = n // 2
                hi, lo = ((w2h, w2l) if n % 2 else (w1h, w1l))
                dve.wait_ge(w_hi, n + 1)
                dve.scalar_tensor_tensor(lo[:, C * p:C * p + C, :], stage[n % STAGES][:], WSCALE,
                                         hi[:, C * p:C * p + C, :], ALU.mult, ALU.subtract).then_inc(w_lo, 1)

            def setup():
                dve.memset(pr_a[:], 0.0).then_inc(zeroed, 1)
                dve.wait_ge(zeroed, 1)
                dve.wait_ge(gate_hi, 1)
                dve.scalar_tensor_tensor(gate_l[:], gate_f[:], WSCALE, gate_h[:], ALU.mult,
                                         ALU.subtract).then_inc(setup_dve, 1)
                dve.wait_ge(setup_pe, 1)
                dve.tensor_copy(cols[:], s3[:, 0:ROWS]).then_inc(setup_dve, 1)
                dve.tensor_copy(gat_wT[:], s2[:, 0:D]).then_inc(setup_dve, 1)
                dve.wait_ge(setup_dve, 3)
                dve.tensor_scalar(b2x[:], cols[:, SLOTS:SLOTS + UNITS], WSCALE, None, ALU.mult).then_inc(setup_dve, 1)
                dve.tensor_scalar(bt_half[:], cols[:, A_ROW + 2:A_ROW + 3], 0.5, None, ALU.mult).then_inc(setup_dve, 1)
                dve.wait_ge(setup_pe, 2)
                dve.tensor_copy(wa[:], s2[:, 0:2]).then_inc(setup_dve, 1)
                dve.wait_ge(setup_dve, 6)
                dve.tensor_copy(wa2_rep[:], wa[:, 1:2].to_broadcast([P, P])).then_inc(setup_dve, 1)

            def stats(i, db, src, st, mv, done):
                for c in range(C):
                    dve.bn_stats(st[:, c, :], src[:, c, :]).then_inc(done, 1)
                for c in range(C):
                    if c == 0:
                        dve.wait_ge(done, count(i, STATS, db, C))
                        dve.memset(carrier[:], 0.0)
                    dve.bn_aggr(mv[:, c, :], st[:, c, :]).then_inc(done, 1)

            def normed(i, db, dst, src, mv, rs, rstd, done):
                dve.wait_ge(rstd, count(i, 2, db, 2))
                for c in range(C):
                    ins = dve.tensor_scalar(dst[:, c, :], src[:, c, :], mv[:, c, 0:1], rs[:, 1, c:c + 1],
                                            ALU.subtract, ALU.mult)
                ins.then_inc(done, 1)

            def softmax_logits(i, db):
                def at(n):
                    return count(i, SOFT, db, n)

                dve.wait_ge(a_s, count(i, 1, db, 1))
                dve.tensor_copy(s1c[:, 0, :], s1[:, 0:C]).then_inc(a_soft, 1)
                s2j = s0[:].rearrange("p (c g n) -> p c g n", c=C, g=gpt)
                for h in range(gpt):
                    ps = slice(h * nodes, (h + 1) * nodes)
                    dve.tensor_reduce(s1c[ps, 1, :], s2j[ps, :, h, :], AX_X, ALU.max).then_inc(a_soft, 1)
                dve.wait_ge(a_soft, at(3))
                for h in range(gpt):
                    ps = slice(h * nodes, (h + 1) * nodes)
                    ins = dve.tensor_tensor(u_a[ps], s2j[ps, :, h, :], bcast(s1c[ps, 0, :], nodes), ALU.add)
                ins.then_inc(a_soft, 1)
                dve.tensor_tensor(s1c[:, 2, :], s1c[:, 0, :], s1c[:, 1, :], ALU.add).then_inc(a_soft, 1)
                dve.wait_ge(a_soft, at(5))
                dve.scalar_tensor_tensor(s1c[:, 3, :], s1c[:, 2, :], ALPHA, s1c[:, 2, :], ALU.mult, ALU.max)\
                   .then_inc(a_soft, 1)
                dve.scalar_tensor_tensor(u_a[:], u_a[:], ALPHA, u_a[:], ALU.mult, ALU.max).then_inc(a_soft, 1)
                dve.wait_ge(a_soft, at(7))
                dve.tensor_tensor(u_a[:], u_a[:], bcast(s1c[:, 3, :], nodes), ALU.subtract).then_inc(a_soft, 1)

            def softmax_numerators(i, db):
                dve.wait_ge(a_exp, count(i, 1, db, 1))
                dve.wait_ge(adja_landed, count(i, 16, db, 16))
                for h in range(gpt):
                    ps = slice(h * nodes, (h + 1) * nodes)
                    ins = dve.scalar_tensor_tensor(pr_a[ps, :, ps], adj_a[ps], 1.0e-6, e_a[ps], ALU.add, ALU.mult)
                ins.then_inc(a_prob, 1)

            def add_attention(i, db):
                dve.wait_ge(a_out, count(i, 1, db, 1))
                dve.reciprocal(rr_a[:], s0[:, 0:C]).then_inc(a_x1n, 1)
                dve.wait_ge(a_x1n, count(i, X1N, db, 1))
                for c in range(C):
                    dve.scalar_tensor_tensor(x1n[:, c, :], s1[:, c * D:(c + 1) * D], rr_a[:, c:c + 1], x_in[:, c, :],
                                             ALU.mult, ALU.add).then_inc(a_x1n, 1)

            def low_parts(i, db, g, bank):
                dve.wait_ge(g.hi_s, count(i, 1, db, 1))
                dve.tensor_tensor(g.lo[:], bank[:], g.hi[:], ALU.subtract).then_inc(g.lo_s, 1)

            def top_two(i, db, g, bank):
                def at(n):
                    return count(i, TOP, db, n)

                ramp_b = ramp[:].unsqueeze(1).to_broadcast([P, C, E])
                logits = bank[:, 0:C * E].rearrange("p (c e) -> p c e", c=C)
                dve.wait_ge(g.logits, count(i, 1, db, 1))
                if g is gates[0]:
                    dve.tensor_scalar(g.lg[:], logits, 1.0 / WSCALE, None, ALU.mult).then_inc(g.top, 1)
                else:
                    dve.scalar_tensor_tensor(g.lg[:], logits, 1.0 / WSCALE,
                                             bg_b[:].unsqueeze(1).to_broadcast([P, C, E]), ALU.mult,
                                             ALU.add).then_inc(g.top, 1)
                n = 1
                for k, src in enumerate((g.lg, g.lg2)):
                    dve.wait_ge(g.top, at(n))
                    dve.tensor_reduce(g.m[:, 2 * k, :], src[:], AX_X, ALU.max).then_inc(g.top, 1)
                    dve.wait_ge(g.top, at(n + 1))
                    dve.tensor_tensor(g.q[:, 2 * k], src[:], bcast(g.m[:, 2 * k, :], E), ALU.is_equal).then_inc(g.top, 1)
                    dve.wait_ge(g.top, at(n + 2))
                    dve.tensor_tensor(g.q[:, 2 * k + 1], g.q[:, 2 * k], ramp_b, ALU.mult).then_inc(g.top, 1)
                    dve.wait_ge(g.top, at(n + 3))
                    dve.tensor_reduce(g.m[:, 2 * k + 1, :], g.q[:, 2 * k + 1], AX_X, ALU.max).then_inc(g.top, 1)
                    dve.wait_ge(g.top, at(n + 4))
                    dve.tensor_tensor(g.one[:, k], g.q[:, 2 * k + 1], bcast(g.m[:, 2 * k + 1, :], E), ALU.is_equal)\
                       .then_inc(g.top, 1)
                    n += 5
                    if k == 0:
                        dve.wait_ge(g.top, at(n))
                        dve.scalar_tensor_tensor(g.lg2[:], g.one[:, 0], NOT_AGAIN, g.lg[:], ALU.mult, ALU.add)\
                           .then_inc(g.top, 1)
                        n += 1
                assert n == 12
                dve.tensor_tensor(g.m[:, 4, :], g.m[:, 2, :], g.m[:, 0, :], ALU.subtract).then_inc(g.top, 1)

            def masks(i, db, g):
                if g is gates[0]:
                    dve.wait_ge(g.tanh, count(i, 1, db, 1))
                    dve.tensor_scalar(g.w[:, 0, :], g.th[:], -0.5, 0.5, ALU.mult, ALU.add).then_inc(g.mask_d, 1)
                    dve.tensor_scalar(g.w[:, 1, :], g.th[:], 0.5, 0.5, ALU.mult, ALU.add).then_inc(g.mask_d, 1)
                    dve.wait_ge(g.mask_d, count(i, 5, db, 2))
                    for k in range(TOPS):
                        dve.tensor_tensor(g.q[:, k], g.one[:, k], bcast(g.w[:, k, :], E), ALU.mult)\
                           .then_inc(g.mask_d, 1)
                    dve.wait_ge(g.mask_d, count(i, 5, db, 4))
                    a, b = g.q[:, 0], g.q[:, 1]
                else:
                    a, b = g.one[:, 0], g.one[:, 1]
                    dve.wait_ge(g.top, count(i, TOP, db, TOP))
                dve.tensor_tensor(g.mask[:].rearrange("p e c -> p c e"), a, b, ALU.add).then_inc(g.mask_d, 1)

            def unit_out(i, u):
                g = gates[0] if u < A_UNITS else gates[1]
                dve.wait_ge(down, chunks(i, LAST[u] + 1))
                y = ps_y[u % 2]
                if u == 0:
                    dve.tensor_scalar(g.acc[:], y[:], b2x[:, 0:1], 1.0 / WSCALE, ALU.add, ALU.mult).then_inc(evac, 1)
                    return
                e = (u - 1) % E
                if e % 2 == 0:
                    dve.wait_ge(g.mb_in[e // 2], count(i, 16, 0 if u < A_UNITS else -1, 16))
                dst = g.acc if u == A_UNITS else scaled
                if dst is scaled:
                    need(dve, summed, sums(i, u))
                dve.scalar_tensor_tensor(dst[:], y[:], b2x[:, u:u + 1], g.mb[:, e, :], ALU.add, ALU.mult)\
                   .then_inc(evac, 1)
                if u != A_UNITS:
                    dve.wait_ge(evac, units(i, u + 1))
                    dve.tensor_tensor(g.acc[:], g.acc[:], scaled[:], ALU.add).then_inc(summed, 1)

            def iteration(i):
                experts0, layer1, next0 = has(i)
                for s in range(SLOTS):
                    if isinstance(i, int) and i == -1 and s == 0:
                        setup()
                    if layer1:
                        if s == 0:
                            dve.wait_ge(x2_made, count(i, 1, -1, 1))
                            stats(i, -1, x2, st_b, mv_b, b_stats)
                            dve.wait_ge(adjb_landed, count(i, 16, -1, 16))
                            dve.tensor_reduce(dg_b[:, 0, :], adj_b[:], AX_X, ALU.add).then_inc(b_deg, 1)
                        if s == 2:
                            normed(i, -1, xn_b, x2, mv_b, rs_b, b_rstd, b_xn)
                        if s == 8:
                            dve.wait_ge(b_f, count(i, 1, -1, 1))
                            dve.wait_ge(b_norm, count(i, 2, -1, 2))
                            dve.tensor_tensor(f_b[:], s3[:].rearrange("p (c d) -> p c d", c=C),
                                              bcast(dg_b[:, 2, :], D), ALU.mult).then_inc(b_fn, 1)
                        if s == 14:
                            dve.wait_ge(b_hom, count(i, 1, -1, 1))
                            dve.wait_ge(b_hets, count(i, 1, -1, 1))
                            dve.tensor_tensor(d_b[:], s3[:], het_b[:], ALU.subtract).then_inc(b_mix, 1)
                            dve.wait_ge(b_mix, count(i, MIX, -1, 1))
                            dve.scalar_tensor_tensor(d_b[:], tg_b[:], 1.0, d_b[:], ALU.add, ALU.mult).then_inc(b_mix, 1)
                            dve.wait_ge(b_mix, count(i, MIX, -1, 2))
                            dve.scalar_tensor_tensor(o_b[:], d_b[:], 0.5, het_b[:], ALU.mult, ALU.add).then_inc(b_mix, 1)
                            dve.wait_ge(b_mix, count(i, MIX, -1, 3))
                            dve.tensor_scalar(d_b[:], o_b[:], 0.0, None, ALU.min).then_inc(b_mix, 1)
                        if s == 16:
                            dve.wait_ge(b_exp, count(i, 1, -1, 1))
                            dve.scalar_tensor_tensor(o_b[:], o_b[:], 0.0, d_b[:], ALU.max, ALU.add).then_inc(b_elu, 1)
                        if s == 19:
                            dve.wait_ge(b_otr, count(i, 1, -1, 1))
                            dve.scalar_tensor_tensor(x3[:], s2[:].rearrange("p (c d) -> p c d", c=C), -1.0, x2[:],
                                                     ALU.add, ALU.add).then_inc(x3_made, 1)
                        if s == 20:
                            dve.wait_ge(x3_made, count(i, 1, -1, 1))
                            stats(i, -1, x3, gates[1].st, gates[1].mv, gates[1].stats)
                        if s == 22:
                            normed(i, -1, gates[1].xn, x3, gates[1].mv, gates[1].rs, gates[1].rstd, gates[1].xn_s)
                        if s == 24:
                            low_parts(i, -1, gates[1], s2)
                        if s == 26:
                            top_two(i, -1, gates[1], s3)
                        if s == 27:
                            masks(i, -1, gates[1])
                    if next0:
                        if s == 3:
                            dve.wait_ge(x_landed, count(i, 16, 1, 16))
                            stats(i, 1, x_in, st_a, mv_a, a_stats)
                        if s == 5:
                            normed(i, 1, xn_a, x_in, mv_a, rs_a, a_rstd, a_xn)
                        if s == 12:
                            softmax_logits(i, 1)
                        if s == 17:
                            softmax_numerators(i, 1)
                        if s == 23:
                            add_attention(i, 1)
                        if s == 30:
                            dve.wait_ge(a_x1n, count(i, X1N, 1, X1N))
                            stats(i, 1, x1n, gates[0].st, gates[0].mv, gates[0].stats)
                        if s == 32:
                            normed(i, 1, gates[0].xn, x1n, gates[0].mv, gates[0].rs, gates[0].rstd, gates[0].xn_s)
                        if s == 37:
                            low_parts(i, 1, gates[0], s0)
                        if s == 40:
                            top_two(i, 1, gates[0], s1)
                        if s == 43:
                            masks(i, 1, gates[0])
                    if (experts0 and s < A_SLOTS) or (layer1 and s >= A_SLOTS):
                        k = s % H_SLOTS
                        dve.wait_ge(gelu, 2 * chunks(i, s + 1))
                        dve.tensor_tensor(hlo[k][:], h32[k][:], hhi[k][:], ALU.subtract).then_inc(low, 1)
                    for u in range(UNITS):
                        if LAST[u] + LAG == s and (experts0 if u < A_UNITS else layer1):
                            unit_out(i, u)
                    if s == 42:
                        if experts0:
                            dve.wait_ge(gates[0].acc_tr, count(i, 1, 0, 1))
                            dve.tensor_tensor(x2[:], s2[:].rearrange("p (c d) -> p c d", c=C), x1[:], ALU.add)\
                               .then_inc(x2_made, 1)
                        if next0:
                            if experts0:
                                dve.wait_ge(x2_made, count(i, 1, 0, 1))
                            else:
                                dve.wait_ge(a_x1n, count(i, X1N, 1, X1N))
                            dve.tensor_copy(x1[:], x1n[:]).then_inc(x1_made, 1)
                    if isinstance(i, int) and i == -1 and s < 2 * PIECES:
                        weight_piece(s)
                if layer1:
                    for u in range(UNITS):
                        if LAST[u] + LAG >= SLOTS:
                            unit_out(i, u)
                    dve.wait_ge(gates[1].acc_tr, count(i, 1, -1, 1))
                    need(dve, stored, count(i, 16, -1, 0))
                    dve.tensor_tensor(x4[:], s2[:].rearrange("p (c d) -> p c d", c=C), x3[:], ALU.add)\
                       .then_inc(x4_made, 1)

            in_blocks(dve, iteration)

        @block.tensor
        def _(pe):
            def transposes(bank, src):
                for c in range(C):
                    ins = pe.transpose(bank[:, c * P:(c + 1) * P], src[:, c * P:(c + 1) * P], ident[:])
                return ins

            def flat(t):
                return t[:].rearrange("p c d -> p (c d)")

            def setup():
                pe.wait_ge(consts, CONSTS)
                pe.wait_ge(small_in, 16 * SMALL)
                pe.transpose(s3[:, 0:ROWS], rows[:], ident[0:ROWS, 0:ROWS])
                pe.transpose(s2[:, 0:D], gat_w[:], ident[:]).then_inc(setup_pe, 1)
                pe.wait_ge(setup_dve, 3)
                pe.matmul(s2[:, 0:2], gat_wT[:], cols[:, A_ROW:A_ROW + 2], start=True, stop=True).then_inc(setup_pe, 1)

            def up_product(i, s):
                g = gates[0] if s < A_SLOTS else gates[1]
                if s == 0 or s == A_SLOTS:
                    pe.wait_ge(g.lo_s, count(i, 1, 0 if s == 0 else -1, 1))
                if isinstance(i, int) and i <= 1:
                    pe.wait_ge(w_lo, min(2 * (s // C + 1), 2 * PIECES))
                need(pe, gelu, 2 * (chunks(i, s - 1)))
                h = ps_h[s % 2]
                pe.matmul(h[:], w1h[:, s, :], g.hi[:], start=True, stop=False)
                pe.matmul(h[:], w1l[:, s, :], g.hi[:], start=False, stop=False)
                pe.matmul(h[:], w1h[:, s, :], g.lo[:], start=False, stop=True).then_inc(up, 1)

            def down_product(i, s):
                u = UNIT_OF[s]
                k = s % H_SLOTS
                y = ps_y[u % 2]
                if s == FIRST[u]:
                    need(pe, evac, units(i, 0) if u == 0 else units(i, u) - 1)
                pe.wait_ge(low, chunks(i, s + 1))
                pe.matmul(y[:], w2h[:, s, :], hhi[k][:], start=(s == FIRST[u]), stop=False)
                pe.matmul(y[:], w2l[:, s, :], hhi[k][:], start=False, stop=False)
                pe.matmul(y[:], w2h[:, s, :], hlo[k][:], start=False, stop=(s == LAST[u])).then_inc(down, 1)

            def logits(i, db, g, n, bank):
                pe.wait_ge(g.lo_s, count(i, 1, db, 1))
                for c in range(C):
                    o = bank[:, c * E:(c + 1) * E]
                    t = slice(c * P, (c + 1) * P)
                    pe.matmul(o, g.hi[:, t], gate_h[:, n, :], start=True, stop=False)
                    pe.matmul(o, g.hi[:, t], gate_l[:, n, :], start=False, stop=False)
                    ins = pe.matmul(o, g.lo[:, t], gate_h[:, n, :], start=False, stop=True)
                ins.then_inc(g.logits, 1)

            def mask_transpose(i, db, g, bank):
                pe.wait_ge(g.mask_d, count(i, 5 if g is gates[0] else 1, db, 5 if g is gates[0] else 1))
                pe.transpose(bank[0:E * C, 0:P], g.mask[:].rearrange("p e c -> p (e c)"), ident[:])\
                  .then_inc(g.mask_tr, 1)

            def iteration(i):
                experts0, layer1, next0 = has(i)
                if isinstance(i, int) and i == -1:
                    setup()
                for s in range(SLOTS):
                    if layer1:
                        if s == 4:
                            pe.wait_ge(b_xn, count(i, 1, -1, 1))
                            transposes(s2, flat(xn_b)).then_inc(b_tr, 1)
                        if s == 6:
                            pe.wait_ge(b_xt, count(i, 1, -1, 1))
                            for c in range(C):
                                ins = pe.matmul(s3[:, c * D:(c + 1) * D], xt_b[:, c * P:(c + 1) * P], theta_w[:],
                                                start=True, stop=True)
                            ins.then_inc(b_f, 1)
                        if s == 8:
                            pe.wait_ge(b_adjn, count(i, 2, -1, 2))
                            transposes(s2, flat(an_b)).then_inc(b_atr, 1)
                        if s == 9:
                            pe.wait_ge(b_fn, count(i, 1, -1, 1))
                            pe.matmul(s3[:], wt_w[:], xt_b[:], start=True, stop=True).then_inc(b_gate, 1)
                        if s == 11:
                            pe.wait_ge(b_at, count(i, 1, -1, 1))
                            pe.matmul(s2[:], wh_w[:], xt_b[:], start=True, stop=True).then_inc(b_het, 1)
                        if s == 12:
                            pe.wait_ge(b_tanh, count(i, 1, -1, 1))
                            for c in range(C):
                                t = slice(c * P, (c + 1) * P)
                                ins = pe.matmul(s3[:, t], f_b[:, c, :], at_b[:, t], start=True, stop=True)
                            ins.then_inc(b_hom, 1)
                        if s == 18:
                            pe.wait_ge(b_elu, count(i, 1, -1, 1))
                            transposes(s2, o_b).then_inc(b_otr, 1)
                        if s == 23:
                            pe.wait_ge(gates[1].xn_s, count(i, 1, -1, 1))
                            transposes(s2, flat(gates[1].xn)).then_inc(gates[1].tr, 1)
                        if s == 25:
                            logits(i, -1, gates[1], 1, s3)
                        if s == 30:
                            mask_transpose(i, -1, gates[1], s3)
                    if next0:
                        if s == 7:
                            pe.wait_ge(a_xn, count(i, 1, 1, 1))
                            transposes(s0, flat(xn_a)).then_inc(a_tr, 1)
                        if s == 10:
                            pe.wait_ge(a_xt, count(i, 1, 1, 1))
                            if isinstance(i, int) and i == -1:
                                pe.wait_ge(setup_dve, 7)
                            for c in range(C):
                                pe.matmul(s1[:, c:c + 1], xt_a[:, c * P:(c + 1) * P], wa[:, 0:1], start=True, stop=True)
                            pe.matmul(s0[:], wa2_rep[:], xt_a[:], start=True, stop=True).then_inc(a_s, 1)
                        if s == 13:
                            pe.wait_ge(a_soft, count(i, SOFT, 1, 1))
                            for c in range(C):
                                ins = pe.matmul(s1[:, c * D:(c + 1) * D], xt_a[:, c * P:(c + 1) * P], gat_w[:],
                                                start=True, stop=True)
                            ins.then_inc(a_wh, 1)
                        if s == 19:
                            pe.wait_ge(a_prob, count(i, 1, 1, 1))
                            transposes(s0, flat(pr_a)).then_inc(a_ptr, 1)
                        if s == 22:
                            pe.wait_ge(a_pt, count(i, 1, 1, 1))
                            pe.wait_ge(a_whs, count(i, 1, 1, 1))
                            for c in range(C):
                                t = slice(c * P, (c + 1) * P)
                                pe.matmul(s0[:, c:c + 1], pt_a[:, t], ones[:, 0:1], start=True, stop=True)
                            for c in range(C):
                                t = slice(c * P, (c + 1) * P)
                                ins = pe.matmul(s1[:, t], pt_a[:, t], wh_a[:, t], start=True, stop=True)
                            ins.then_inc(a_out, 1)
                        if s == 34:
                            pe.wait_ge(gates[0].xn_s, count(i, 1, 1, 1))
                            transposes(s0, flat(gates[0].xn)).then_inc(gates[0].tr, 1)
                        if s == 39:
                            logits(i, 1, gates[0], 0, s1)
                        if s == 45:
                            mask_transpose(i, 1, gates[0], s1)
                    if experts0 and s == 41:
                        pe.wait_ge(summed, sums(i, A_UNITS))
                        transposes(s2, gates[0].acc).then_inc(gates[0].acc_tr, 1)
                    if (experts0 and s < A_SLOTS) or (layer1 and s >= A_SLOTS):
                        up_product(i, s)
                    t = s - LAG
                    if t >= 0 and ((experts0 and t < A_SLOTS) or (layer1 and t >= A_SLOTS)):
                        down_product(i, t)
                if layer1:
                    for t in range(SLOTS - LAG, SLOTS):
                        down_product(i, t)
                    pe.wait_ge(summed, sums(i, UNITS))
                    transposes(s2, gates[1].acc).then_inc(gates[1].acc_tr, 1)

            in_blocks(pe, iteration)


_NAMES = ["x", "adj", "L0_gnn_W", "L0_gnn_a", "L0_ffn_Wr", "L0_ffn_W1s", "L0_ffn_b1s", "L0_ffn_W2s", "L0_ffn_b2s",
          "L0_ffn_W1p", "L0_ffn_b1p", "L0_ffn_W2p", "L0_ffn_b2p", "L1_gnn_W_t", "L1_gnn_b_t", "L1_gnn_W_h",
          "L1_gnn_theta", "L1_ffn_Wg", "L1_ffn_bg", "L1_ffn_W1", "L1_ffn_b1", "L1_ffn_W2", "L1_ffn_b2"]


def kernel(**inputs):
    import numpy as np
    import concourse.bacc as bacc
    from concourse.bass_utils import run_bass_kernel_spmd

    nc = bacc.Bacc("TRN2", target_bir_lowering=False, num_devices=1)
    arrays, args = {}, []
    for name in _NAMES:
        a = np.ascontiguousarray(inputs[name])
        arrays[f"in_{name}"] = a
        args.append(nc.dram_tensor(f"in_{name}", a.shape, mybir.dt.from_np(a.dtype), kind="ExternalInput").ap())
    args.append(nc.dram_tensor("result", inputs["x"].shape, F32, kind="ExternalOutput").ap())
    mk_adj_ffn_kernel(nc, *args)
    r = run_bass_kernel_spmd(nc, [arrays], core_ids=[0])
    return r.results[0]["result"]
```

```python
from contextlib import ExitStack

import concourse.bass as bass
from concourse import mybir

F32 = mybir.dt.float32
F16 = mybir.dt.float16
ALU = mybir.AluOpType
ACT = mybir.ActivationFunctionType
AX_X = mybir.AxisListType.X

P = 128
D = 128
C = 4
BLK = C * P
E = 8
TOPS = 2
WSCALE = 256.0
ALPHA = 0.2
NOT_AGAIN = -1.0e30

H_SLOTS = 4
LAG = 3
WHOLE = (10, 13, 37, 41, 50)

BY_POOL = (17, 28, 42)
PIECE_AT = (0, 3, 6, 9, 10, 11, 16, 17, 21, 22, 27, 30, 53, 56, 58, 60, 62, 64, 66, 68, 70, 72, 74, 75, 75, 77)

PE_AT = {
    "f": 3, "adj_tr": 3, "gate_b": 3, "acc1_tr": 5, "het": 7, "hom": 8, "xa_tr": 9, "scores": 11, "wh": 11,
    "o_tr": 16, "p_tr": 19, "out": 21, "xn1_tr": 24, "logits_1": 30, "xn0_tr": 32, "logits_0": 37, "mask1_tr": 38,
    "acc0_tr": 42, "mask0_tr": 47, "xb_tr": 51,
}
ACT_AT = {
    "at_b": 3, "tanh_b": 4, "het_copy": 7, "xt_a": 8, "wh_copy": 11, "exp_b": 14, "exp_a": 14, "pt_copy": 19,
    "hi_1": 25, "hi_0": 32, "rows_1": 38, "tanh_0": 40, "rows_0": 47, "xt_b": 51,
}
DVE_AT = {
    "stats_a": 0, "f_b": 4, "x4": 4, "norm_a": 5, "mix_1": 8, "mix_2": 8, "mix_3": 9, "softmax": (10, 11), "elu": 13,
    "numerators": 14, "x3": 17, "stats_1": 19, "norm_1": 21, "attend": 24, "stats_0": 24, "low_1": 25, "norm_0": 28,
    "top_1": (30, 33, 35), "low_0": 33, "masks_1": 35, "top_0": (35, 36, 37), "move_0": 39, "masks_0": 42, "x2": 42,
    "x1": 44, "norm_b": 48,
}
POOL_AT = {
    "rstd_a": 0, "rstd_1": 20, "rstd_0": 26, "rstd_b": 45, "adj_norm": 47,
}


def mk_adj_ffn_kernel(
    nc, x, adj, gat_W, gat_a, Wr, W1s, b1s, W2s, b2s, W1p, b1p, W2p, b2p,
    W_t, b_t, W_h, theta, Wg, bg, W1, b1, W2, b2, out,
):
    graphs, nodes, _ = x.shape
    gpt = P // nodes
    NB = graphs * nodes // BLK
    SH = W1s.shape[1] // P
    K0 = W1p.shape[2] // P
    K1 = W1.shape[2] // P
    A_SLOTS = SH + E * K0
    SLOTS = A_SLOTS + E * K1
    UNIT_LEN = [SH] + [K0] * E + [K1] * E
    UNITS = len(UNIT_LEN)
    A_UNITS = 1 + E
    UNIT_OF = [u for u, k in enumerate(UNIT_LEN) for _ in range(k)]
    FIRST = [sum(UNIT_LEN[:u]) for u in range(UNITS)]
    LAST = [sum(UNIT_LEN[:u + 1]) - 1 for u in range(UNITS)]
    assert gpt == 2 and A_SLOTS % H_SLOTS == 0 and SLOTS % H_SLOTS == 0 and SH == K0

    def count(i, per_block, db, n):
        return per_block * i + (per_block * db + n)

    def before(i, n, in_layer0, in_all, back=0):
        if isinstance(i, int):
            i, back = i - back, 0
            if i == 0:
                return n
            if i == NB:
                n -= in_layer0
        return in_all * i + (in_layer0 - in_all + n - in_all * back)

    def chunks(i, s, back=0):
        return before(i, s, A_SLOTS, SLOTS, back)

    def lows(i, s, by_pool, back=0):
        def split(n):
            return sum((c in BY_POOL) == by_pool for c in range(n) if c not in WHOLE)

        return before(i, split(s), split(A_SLOTS), split(SLOTS), back)

    def units(i, u, back=0):
        return before(i, u, A_UNITS, UNITS, back)

    def sums(i, u, back=0):
        return before(i, max(u - 1, 0) - (1 if u > A_UNITS else 0), E, 2 * E - 1, back)

    H_BANK = [s % 3 for s in range(SLOTS - 1)] + [1]

    def bank_free(i, s):
        near = s in (1, SLOTS - 1) or (isinstance(i, int) and i == NB)
        return chunks(i, s) - (1 if near else 2)

    def need(eng, sem, value):
        if not isinstance(value, int) or value > 0:
            eng.wait_ge(sem, value)

    def in_blocks(eng, body, last=2):
        body(-1)
        body(0)
        body(1)
        with eng.Fori(2, NB + 1 - last) as i:
            body(i)
        for i in range(NB + 1 - last, NB + 1):
            body(i)

    def has(i):
        if not isinstance(i, int):
            return True, True, True, True
        return 0 <= i < NB, 1 <= i <= NB, i + 1 < NB, 2 <= i <= NB

    x_v = x.rearrange("(b c g) n d -> b (g n) c d", c=C, g=gpt)
    out_v = out.rearrange("(b c g) n d -> b (g n) c d", c=C, g=gpt)
    adj_v = adj.rearrange("(b c g) n m -> b (g n) c m", c=C, g=gpt)

    def block_of(view, b):
        return view[b] if isinstance(b, int) else view[bass.ds(b, 1)].rearrange("b p c d -> (b p) c d")

    with ExitStack() as ctx:
        def sb(name, shape, dt=F32):
            return ctx.enter_context(nc.sbuf_tensor(name, shape, dt))

        def sem(name):
            return ctx.enter_context(nc.semaphore(name))

        ps_h = [ctx.enter_context(nc.psum_tensor(f"ps_h{k}", [P, BLK], F32)) for k in range(3)]
        ps_y = [ctx.enter_context(nc.psum_tensor(f"ps_y{k}", [P, BLK], F32)) for k in range(2)]
        s0, s1, s2 = (ctx.enter_context(nc.psum_tensor(f"ps_s{k}", [P, BLK], F32)) for k in range(3))

        w1h = sb("w1h", [P, SLOTS, P], F16)
        w1l = sb("w1l", [P, SLOTS, P], F16)
        w2h = sb("w2h", [P, SLOTS, P], F16)
        w2l = sb("w2l", [P, SLOTS, P], F16)
        w2f = sb("w2f", [P, len(WHOLE), P])
        PIECES = SLOTS // C
        STAGES = 8
        stage = [sb(f"stage{k}", [P, C, P]) for k in range(STAGES)]
        gat_w = sb("gat_w", [P, D])
        theta_w = sb("theta_w", [P, D])
        wh_w = sb("wh_w", [P, D])
        wt_w = sb("wt_w", [P, D])
        gate_f = sb("gate_f", [P, 2, E])
        gate_h = sb("gate_h", [P, 2, E], F16)
        gate_l = sb("gate_l", [P, 2, E], F16)
        ROWS = SLOTS + UNITS + 3
        A_ROW = SLOTS + UNITS
        rows = sb("rows", [ROWS, P])
        cols = sb("cols", [P, ROWS])
        b2x = sb("b2x", [P, UNITS])
        bt_half = sb("bt_half", [P, 1])
        gat_wT = sb("gat_wT", [P, D])
        wa = sb("wa", [P, 2])
        wa2_rep = sb("wa2_rep", [P, P])
        bg_b = sb("bg_b", [P, E])
        ident = sb("ident", [P, P])
        ones = sb("ones", [P, P])
        ramp = sb("ramp", [P, E])
        neg_half = sb("neg_half", [P, C])
        carrier = sb("carrier", [P, 1])
        eps = sb("eps", [P, 2, C])

        x_in = sb("x_in", [P, C, D])
        adj_a = sb("adj_a", [P, C, nodes])
        st_a = sb("st_a", [P, C, 6])
        mv_a = sb("mv_a", [P, C, 2])
        rs_a = sb("rs_a", [P, 2, C])
        xn_a = sb("xn_a", [P, C, D])
        xt_a = sb("xt_a", [P, BLK])
        s1c = sb("s1c", [P, 4, C])
        u_a = sb("u_a", [P, C, nodes])
        e_a = sb("e_a", [P, C, nodes])
        pr_a = sb("pr_a", [P, C, P])
        pt_a = sb("pt_a", [P, BLK])
        wh_a = sb("wh_a", [P, BLK])
        rr_a = sb("rr_a", [P, C])
        x1n = sb("x1n", [P, C, D])
        x1 = sb("x1", [P, C, D])
        adj_b = sb("adj_b", [P, C, nodes])
        st_b = sb("st_b", [P, C, 6])
        mv_b = sb("mv_b", [P, C, 2])
        rs_b = sb("rs_b", [P, 2, C])
        dg_b = sb("dg_b", [P, 3, C])
        an_b = sb("an_b", [P, C, P])
        at_b = sb("at_b", [P, BLK])
        xn_b = sb("xn_b", [P, C, D])
        xt_b = sb("xt_b", [P, BLK])
        f_b = sb("f_b", [P, C, D])
        tg_b = sb("tg_b", [P, BLK])
        het_b = sb("het_b", [P, BLK])
        d_b = sb("d_b", [P, BLK])
        o_b = sb("o_b", [P, BLK])
        x2 = sb("x2", [P, C, D])
        x3 = sb("x3", [P, C, D])
        x4 = sb("x4", [P, C, D])

        class Gate:
            def __init__(self, n):
                self.st = sb(f"st_f{n}", [P, C, 6])
                self.mv = sb(f"mv_f{n}", [P, C, 2])
                self.rs = sb(f"rs_f{n}", [P, 2, C])
                self.xn = sb(f"xn_f{n}", [P, C, D])
                self.xt = sb(f"xt{n}", [P, 2, BLK], F16)
                if n == 0:
                    self.next = sb("xt_next", [P, 2, BLK], F16)
                self.lg = sb(f"lg{n}", [P, C, E])
                self.lg2 = sb(f"lg2{n}", [P, C, E])
                self.q = sb(f"q{n}", [P, 4, C, E])
                self.one = sb(f"one{n}", [P, 2, C, E])
                self.m = sb(f"m{n}", [P, 5, C])
                self.th = sb(f"th{n}", [P, C])
                self.w = sb(f"w{n}", [P, 2, C])
                self.mask = sb(f"mask{n}", [P, E, C])
                self.mt = sb(f"mt{n}", [E * C, P])
                self.mb = sb(f"mb{n}", [P, E, BLK])
                self.dram = nc.dram_tensor(f"mask_rows{n}", (E * C, P), F32, kind="Internal").ap()
                self.acc = sb(f"acc{n}", [P, BLK])
                self.stats, self.rstd, self.xn_s, self.tr, self.hi_s, self.lo_s, self.logits = (
                    sem(f"{s}{n}") for s in ("stats", "rstd", "xn", "tr", "hi", "lo", "logits"))
                self.top, self.tanh, self.mask_d, self.mask_tr, self.mask_row, self.acc_tr = (
                    sem(f"{s}{n}") for s in ("top", "tanh", "mask_d", "mask_tr", "mask_row", "acc_tr"))
                self.moved = sem(f"moved{n}")
                self.row_out = sem(f"mask_out{n}")
                self.mb_in = [sem(f"mask_in{n}_{k}") for k in range(E // 2)]

        gates = [Gate(0), Gate(1)]
        scaled = sb("scaled", [P, BLK])
        h32 = [sb(f"h32_{k}", [P, BLK]) for k in range(H_SLOTS)]
        hhi = [sb(f"hhi_{k}", [P, BLK], F16) for k in range(H_SLOTS)]
        hlo = [sb(f"hlo_{k}", [P, BLK], F16) for k in range(H_SLOTS)]

        small_in = sem("small_in")
        stage_in = [sem(f"stage_in{k}") for k in range(STAGES)]
        w_hi = sem("w_hi")
        w_lo = sem("w_lo")
        consts = sem("consts")
        zeroed = sem("zeroed")
        setup_pe = sem("setup_pe")
        setup_dve = sem("setup_dve")
        gate_hi = sem("gate_hi")

        x_landed, adja_landed, adjb_landed, stored = sem("x_landed"), sem("adja_landed"), sem("adjb_landed"), sem("stored")
        a_stats, a_rstd, a_xn, a_tr, a_xt = (sem(n) for n in ("a_stats", "a_rstd", "a_xn", "a_tr", "a_xt"))
        a_s, a_soft, a_exp, a_prob, a_ptr, a_pt, a_wh, a_whs, a_out, a_x1n, x1_made = (sem(n) for n in (
            "a_s", "a_soft", "a_exp", "a_prob", "a_ptr", "a_pt", "a_wh", "a_whs", "a_out", "a_x1n", "x1_made"))
        b_stats, b_rstd, b_xn, b_tr, b_xt, b_deg, b_norm, b_adjn = (sem(n) for n in (
            "b_stats", "b_rstd", "b_xn", "b_tr", "b_xt", "b_deg", "b_norm", "b_adjn"))
        b_f, b_fn, b_atr, b_at, b_gate, b_tanh, b_het, b_hets, b_hom, b_mix, b_exp, b_elu, b_otr, x3_made = (
            sem(n) for n in ("b_f", "b_fn", "b_atr", "b_at", "b_gate", "b_tanh", "b_het", "b_hets", "b_hom",
                             "b_mix", "b_exp", "b_elu", "b_otr", "x3_made"))
        x2_made, x4_made = sem("x2_made"), sem("x4_made")
        up = sem("up")
        gelu = sem("gelu")
        low = sem("low")
        low_pool = sem("low_pool")
        down = sem("down")
        evac = sem("evac")
        summed = sem("summed")
        SMALL = 15
        CONSTS = 7 + E

        STATS, SOFT, TOP, X1N, MIX = 2 * C, 8, 13, C + 1, 4

        def bcast(ap, n):
            return ap.unsqueeze(2).to_broadcast([ap.shape[0], ap.shape[1], n])

        block = ctx.enter_context(nc.Block())

        @block.sync
        def _(sp):
            for dst, src in (
                (gat_w[:], gat_W), (theta_w[:], theta), (wh_w[:], W_h), (wt_w[:], W_t),
                (gate_f[:, 0], Wr), (gate_f[:, 1], Wg),
                (rows[0:SH], b1s.rearrange("(k p) -> k p", p=P)),
                (rows[SH:A_SLOTS], b1p.rearrange("e (k p) -> (e k) p", p=P)),
                (rows[A_SLOTS:SLOTS], b1.rearrange("e (k p) -> (e k) p", p=P)),
                (rows[SLOTS:SLOTS + 1], b2s.rearrange("(k p) -> k p", p=P)),
                (rows[SLOTS + 1:SLOTS + 1 + E], b2p), (rows[SLOTS + 1 + E:SLOTS + UNITS], b2),
                (rows[A_ROW:A_ROW + 2], gat_a.rearrange("(k p) u -> k (p u)", p=P)),
                (rows[A_ROW + 2:A_ROW + 3], b_t.rearrange("(k p) -> k p", p=P)),
                (bg_b[:], bg.rearrange("(u e) -> u e", u=1).to_broadcast([P, E])),
            ):
                sp.dma_start(dst, src).then_inc(small_in, 16)

            def weight_pieces(some):
                for n in some:
                    p, second = n // 2, n % 2
                    if n >= STAGES:
                        sp.wait_ge(w_lo, n - STAGES + 1)
                    if p == 0:
                        src = W2s.rearrange("(k p) d -> p k d", p=P) if second else W1s.rearrange("d (k p) -> d k p", p=P)
                        sp.dma_start(stage[n % STAGES][:], src).then_inc(stage_in[n % STAGES], 16)
                    elif p <= E:
                        src = (W2p[p - 1].rearrange("(k p) d -> p k d", p=P) if second
                               else W1p[p - 1].rearrange("d (k p) -> d k p", p=P))
                        sp.dma_start(stage[n % STAGES][:], src).then_inc(stage_in[n % STAGES], 16)
                    else:
                        e = (p - 1 - E) * (C // K1)
                        for j in range(C // K1):
                            src = (W2[e + j].rearrange("(k p) d -> p k d", p=P) if second
                                   else W1[e + j].rearrange("d (k p) -> d k p", p=P))
                            sp.dma_start(stage[n % STAGES][:, j * K1:(j + 1) * K1], src)\
                              .then_inc(stage_in[n % STAGES], 16)

            def masks_out(i, db, g):
                sp.wait_ge(g.mask_row, count(i, 1, db, 1))
                sp.dma_start(g.dram, g.mt[:]).then_inc(g.row_out, 16)
                sp.wait_ge(g.row_out, count(i, 16, db, 16))
                for k in range(E // 2):
                    src = g.dram[2 * k * C:2 * (k + 1) * C].rearrange("(u r) p -> u (r p)", u=1)
                    sp.dma_start(g.mb[:, 2 * k:2 * k + 2, :].rearrange("p e t -> p (e t)"),
                                 src.to_broadcast([P, 2 * BLK])).then_inc(g.mb_in[k], 16)

            def iteration(i):
                experts0, layer1, next0, last1 = has(i)
                if isinstance(i, int) and i == -1:
                    load(i, 1)
                if experts0:
                    src_b = block_of(adj_v, i)
                    need(sp, b_adjn, count(i, 2, 0, 0))
                    sp.dma_start(adj_b[:], src_b).then_inc(adjb_landed, 16)
                if last1:
                    store(i, -2)
                early = min(sum(slot < SLOTS for slot in PIECE_AT) + STAGES, 2 * PIECES)
                if isinstance(i, int) and i == -1:
                    weight_pieces(range(early))
                if isinstance(i, int) and i == 0:
                    weight_pieces(range(early, 2 * PIECES))
                if layer1:
                    masks_out(i, -1, gates[1])
                if not isinstance(i, int) or i + 2 < NB:
                    load(i, 2)
                if next0:
                    masks_out(i, 1, gates[0])

            def load(i, db):
                src_x, src_a = block_of(x_v, i + db), block_of(adj_v, i + db)
                need(sp, a_x1n, count(i, X1N, db, 0))
                sp.dma_start(x_in[:], src_x).then_inc(x_landed, 16)
                sp.dma_start(adj_a[:], src_a).then_inc(adja_landed, 16)

            def store(i, db):
                dst = block_of(out_v, i + db)
                sp.wait_ge(x4_made, count(i, 1, db, 1))
                sp.dma_start(dst, x4[:]).then_inc(stored, 16)

            in_blocks(sp, iteration, 3)
            store(NB, -1)
            sp.wait_ge(stored, 16 * NB)

        @block.gpsimd
        def _(pool):
            pool.memset(ident[:], 0.0).then_inc(consts, 1)
            pool.memset(ones[:], 1.0).then_inc(consts, 1)
            pool.memset(neg_half[:], -0.5).then_inc(consts, 1)
            pool.memset(eps[:, 0, :], 1.0e-5).then_inc(consts, 1)
            pool.memset(eps[:, 1, :], 1.0e-6).then_inc(consts, 1)
            for e in range(E):
                pool.memset(ramp[:, e:e + 1], float(E - e)).then_inc(consts, 1)
            pool.memset(an_b[:], 0.0).then_inc(consts, 1)
            pool.wait_ge(consts, 1)
            pool.affine_select(out=ident[:], in_=ident[:], compare_op=ALU.not_equal, fill=1.0,
                               base=0, pattern=[[-1, P]], channel_multiplier=1).then_inc(consts, 1)
            pool.wait_ge(consts, CONSTS)

            def rstd(i, db, mv, rs, stats, done):
                pool.wait_ge(stats, count(i, STATS, db, STATS))
                pool.tensor_tensor(rs[:, 0, :], mv[:, :, 1], eps[:, 0, :], ALU.add).then_inc(done, 1)
                pool.wait_ge(done, count(i, 2, db, 1))
                pool.tensor_tensor(rs[:, 1, :], rs[:, 0, :], neg_half[:], ALU.pow).then_inc(done, 1)

            def adj_norm(i, db):
                pool.wait_ge(b_deg, count(i, 1, db, 1))
                pool.tensor_tensor(dg_b[:, 1, :], dg_b[:, 0, :], eps[:, 1, :], ALU.add).then_inc(b_norm, 1)
                pool.wait_ge(b_norm, count(i, 2, db, 1))
                pool.tensor_tensor(dg_b[:, 2, :], dg_b[:, 1, :], neg_half[:], ALU.pow).then_inc(b_norm, 1)
                pool.wait_ge(b_norm, count(i, 2, db, 2))
                need(pool, b_at, count(i, 1, db, 0))
                for h in range(gpt):
                    ps = slice(h * nodes, (h + 1) * nodes)
                    pool.tensor_tensor(an_b[ps, :, ps], adj_b[ps, :, :], bcast(dg_b[ps, 2, :], nodes),
                                       ALU.mult).then_inc(b_adjn, 1)
                    pool.wait_ge(b_adjn, count(i, 2, db, h + 1))

            def unit_add(i, u, back=0):
                if u == 0 or u == A_UNITS:
                    return
                g = gates[0] if u < A_UNITS else gates[1]
                pool.wait_ge(evac, units(i, u + 1, back))
                pool.tensor_tensor(g.acc[:], g.acc[:], scaled[:], ALU.add).then_inc(summed, 1)

            def iteration(i):
                experts0, layer1, next0, last1 = has(i)
                for s in range(SLOTS):
                    if next0 and s == POOL_AT["rstd_a"]:
                        rstd(i, 1, mv_a, rs_a, a_stats, a_rstd)
                    if layer1 and s == POOL_AT["rstd_1"]:
                        rstd(i, -1, gates[1].mv, gates[1].rs, gates[1].stats, gates[1].rstd)
                    if next0 and s == POOL_AT["rstd_0"]:
                        rstd(i, 1, gates[0].mv, gates[0].rs, gates[0].stats, gates[0].rstd)
                    if experts0 and s == POOL_AT["rstd_b"]:
                        rstd(i, 0, mv_b, rs_b, b_stats, b_rstd)
                    if experts0 and s == POOL_AT["adj_norm"]:
                        adj_norm(i, 0)
                    if ((experts0 and s < A_SLOTS) or (layer1 and s >= A_SLOTS)) and s in BY_POOL:
                        k = s % H_SLOTS
                        pool.wait_ge(gelu, chunks(i, s + 1))
                        pool.tensor_tensor(hlo[k][:], h32[k][:], hhi[k][:], ALU.subtract).then_inc(low_pool, 1)
                    for u in range(UNITS):
                        if LAST[u] + LAG == s and (experts0 if u < A_UNITS else layer1):
                            unit_add(i, u)
                        if LAST[u] + LAG == s + SLOTS and last1:
                            unit_add(i, u, 1)
                if isinstance(i, int) and i == NB:
                    for u in range(UNITS):
                        if LAST[u] + LAG >= SLOTS:
                            unit_add(i, u)

            in_blocks(pool, iteration)

        @block.scalar
        def _(act):
            def weight_piece(n):
                p = n // 2
                hi = (w2h if n % 2 else w1h)[:, C * p:C * p + C, :]
                halves = 1 if p <= E else C // K1
                before = sum(16 * (1 if m // 2 <= E else C // K1) for m in range(n % STAGES, n, STAGES))
                act.wait_ge(stage_in[n % STAGES], before + 16 * halves)
                act.activation(hi, stage[n % STAGES][:], ACT.Copy, scale=WSCALE).then_inc(w_hi, 1)

            def setup():
                act.wait_ge(small_in, 16 * SMALL)
                act.activation(gate_h[:], gate_f[:], ACT.Copy, scale=WSCALE).then_inc(gate_hi, 1)

            def copy_out(i, db, dst, src, ready, done, free=None):
                act.wait_ge(ready, count(i, 1, db, 1))
                if free is not None:
                    need(act, *free)
                act.activation(dst, src, ACT.Copy).then_inc(done, 1)

            def gate_tanh(i, db, g):
                act.wait_ge(g.top, count(i, TOP, db, TOP))
                act.activation(g.th[:], g.m[:, 4, :], ACT.Tanh, scale=0.5).then_inc(g.tanh, 1)

            def mask_rows(i, db, g, units_before):
                need(act, evac, units_before)
                act.wait_ge(g.mask_tr, count(i, 1, db, 1))
                need(act, g.row_out, count(i, 16, db, 0))
                act.activation(g.mt[:], (s1 if g is gates[0] else s2)[0:E * C, 0:P], ACT.Copy,
                               scale=1.0 / WSCALE).then_inc(g.mask_row, 1)

            def iteration(i):
                experts0, layer1, next0, last1 = has(i)
                for s in range(SLOTS):
                    if layer1:
                        if s == ACT_AT["at_b"]:
                            copy_out(i, -1, at_b[:], s2[:], b_atr, b_at)
                        if s == ACT_AT["tanh_b"]:
                            act.wait_ge(b_gate, count(i, 1, -1, 1))
                            act.activation(tg_b[:], s0[:], ACT.Tanh, bias=bt_half[:, 0:1], scale=0.5)\
                               .then_inc(b_tanh, 1)
                        if s == ACT_AT["het_copy"]:
                            copy_out(i, -1, het_b[:], s1[:], b_het, b_hets)
                        if s == ACT_AT["exp_b"]:
                            act.wait_ge(b_mix, count(i, MIX, -1, MIX))
                            act.activation(d_b[:], d_b[:], ACT.Exp).then_inc(b_exp, 1)
                        if s == ACT_AT["hi_1"]:
                            copy_out(i, -1, gates[1].xt[:, 0, :], s1[:], gates[1].tr, gates[1].hi_s)
                        if s == ACT_AT["rows_1"]:
                            mask_rows(i, -1, gates[1], units(i, 0) if experts0 else units(i, A_UNITS))
                    if next0:
                        if s == ACT_AT["xt_a"]:
                            copy_out(i, 1, xt_a[:], s0[:], a_tr, a_xt)
                        if s == ACT_AT["wh_copy"]:
                            copy_out(i, 1, wh_a[:], s2[:], a_wh, a_whs)
                        if s == ACT_AT["exp_a"]:
                            act.wait_ge(a_soft, count(i, SOFT, 1, SOFT))
                            act.activation(e_a[:], u_a[:], ACT.Exp).then_inc(a_exp, 1)
                        if s == ACT_AT["pt_copy"]:
                            copy_out(i, 1, pt_a[:], s0[:], a_ptr, a_pt)
                        if s == ACT_AT["hi_0"]:
                            copy_out(i, 1, gates[0].next[:, 0, :], s0[:], gates[0].tr, gates[0].hi_s)
                        if s == ACT_AT["tanh_0"]:
                            gate_tanh(i, 1, gates[0])
                        if s == ACT_AT["rows_0"]:
                            mask_rows(i, 1, gates[0], units(i, A_UNITS) if experts0 else 0)
                    if experts0 and s == ACT_AT["xt_b"]:
                        copy_out(i, 0, xt_b[:], s1[:], b_tr, b_xt)
                    if (experts0 and s < A_SLOTS) or (layer1 and s >= A_SLOTS):
                        k = s % H_SLOTS
                        act.wait_ge(up, chunks(i, s + 1))
                        need(act, down, chunks(i, s + 1) - H_SLOTS)
                        ins = act.activation(h32[k][:], ps_h[H_BANK[s]][:], ACT.Gelu, bias=cols[:, s:s + 1],
                                             scale=1.0 / WSCALE)
                        if s not in WHOLE:
                            ins = act.activation(hhi[k][:], ps_h[H_BANK[s]][:], ACT.Gelu, bias=cols[:, s:s + 1],
                                                 scale=1.0 / WSCALE)
                        ins.then_inc(gelu, 1)
                    if isinstance(i, int) and i < 1:
                        if i == -1 and s == 0:
                            setup()
                        for n in range(2 * PIECES):
                            if PIECE_AT[n] == (i + 1) * SLOTS + s:
                                weight_piece(n)

            in_blocks(act, iteration)

        @block.vector
        def _(dve):
            def weight_piece(n):
                p = n // 2
                hi, lo = ((w2h, w2l) if n % 2 else (w1h, w1l))
                dve.wait_ge(w_hi, n + 1)
                for j, w in enumerate(WHOLE):
                    if n % 2 and w // C == p:
                        dve.tensor_scalar(w2f[:, j, :], stage[n % STAGES][:, w % C, :], WSCALE, None, ALU.mult)
                dve.scalar_tensor_tensor(lo[:, C * p:C * p + C, :], stage[n % STAGES][:], WSCALE,
                                         hi[:, C * p:C * p + C, :], ALU.mult, ALU.subtract).then_inc(w_lo, 1)

            def setup():
                dve.memset(pr_a[:], 0.0).then_inc(zeroed, 1)
                dve.wait_ge(zeroed, 1)
                dve.wait_ge(gate_hi, 1)
                dve.scalar_tensor_tensor(gate_l[:], gate_f[:], WSCALE, gate_h[:], ALU.mult,
                                         ALU.subtract).then_inc(setup_dve, 1)
                dve.wait_ge(setup_pe, 1)
                dve.tensor_copy(cols[:], s1[:, 0:ROWS]).then_inc(setup_dve, 1)
                dve.tensor_copy(gat_wT[:], s2[:, 0:D]).then_inc(setup_dve, 1)
                dve.wait_ge(setup_dve, 3)
                dve.tensor_scalar(b2x[:], cols[:, SLOTS:SLOTS + UNITS], WSCALE, None, ALU.mult).then_inc(setup_dve, 1)
                dve.tensor_scalar(bt_half[:], cols[:, A_ROW + 2:A_ROW + 3], 0.5, None, ALU.mult).then_inc(setup_dve, 1)
                dve.wait_ge(setup_pe, 2)
                dve.tensor_copy(wa[:], s2[:, 0:2]).then_inc(setup_dve, 1)
                dve.wait_ge(setup_dve, 6)
                dve.tensor_copy(wa2_rep[:], wa[:, 1:2].to_broadcast([P, P])).then_inc(setup_dve, 1)

            def stats(i, db, src, st, mv, done):
                for c in range(C):
                    dve.bn_stats(st[:, c, :], src[:, c, :]).then_inc(done, 1)
                for c in range(C):
                    if c == 0:
                        dve.wait_ge(done, count(i, STATS, db, C))
                        dve.memset(carrier[:], 0.0)
                    dve.bn_aggr(mv[:, c, :], st[:, c, :]).then_inc(done, 1)

            def normed(i, db, dst, src, mv, rs, rstd, done):
                dve.wait_ge(rstd, count(i, 2, db, 2))
                for c in range(C):
                    ins = dve.tensor_scalar(dst[:, c, :], src[:, c, :], mv[:, c, 0:1], rs[:, 1, c:c + 1],
                                            ALU.subtract, ALU.mult)
                ins.then_inc(done, 1)

            def softmax_logits(i, db, part):
                def at(n):
                    return count(i, SOFT, db, n)

                if part == 1:
                    dve.wait_ge(a_soft, at(5))
                    dve.scalar_tensor_tensor(s1c[:, 3, :], s1c[:, 2, :], ALPHA, s1c[:, 2, :], ALU.mult, ALU.max)\
                       .then_inc(a_soft, 1)
                    dve.scalar_tensor_tensor(u_a[:], u_a[:], ALPHA, u_a[:], ALU.mult, ALU.max).then_inc(a_soft, 1)
                    dve.wait_ge(a_soft, at(7))
                    dve.tensor_tensor(u_a[:], u_a[:], bcast(s1c[:, 3, :], nodes), ALU.subtract).then_inc(a_soft, 1)
                    return
                dve.wait_ge(a_s, count(i, 1, db, 1))
                dve.tensor_copy(s1c[:, 0, :], s1[:, 0:C]).then_inc(a_soft, 1)
                s2j = s0[:].rearrange("p (c g n) -> p c g n", c=C, g=gpt)
                for h in range(gpt):
                    ps = slice(h * nodes, (h + 1) * nodes)
                    dve.tensor_reduce(s1c[ps, 1, :], s2j[ps, :, h, :], AX_X, ALU.max).then_inc(a_soft, 1)
                dve.wait_ge(a_soft, at(3))
                for h in range(gpt):
                    ps = slice(h * nodes, (h + 1) * nodes)
                    ins = dve.tensor_tensor(u_a[ps], s2j[ps, :, h, :], bcast(s1c[ps, 0, :], nodes), ALU.add)
                ins.then_inc(a_soft, 1)
                dve.tensor_tensor(s1c[:, 2, :], s1c[:, 0, :], s1c[:, 1, :], ALU.add).then_inc(a_soft, 1)

            def softmax_numerators(i, db):
                dve.wait_ge(a_exp, count(i, 1, db, 1))
                dve.wait_ge(adja_landed, count(i, 16, db, 16))
                for h in range(gpt):
                    ps = slice(h * nodes, (h + 1) * nodes)
                    ins = dve.scalar_tensor_tensor(pr_a[ps, :, ps], adj_a[ps], 1.0e-6, e_a[ps], ALU.add, ALU.mult)
                ins.then_inc(a_prob, 1)

            def add_attention(i, db):
                dve.wait_ge(a_out, count(i, 1, db, 1))
                dve.reciprocal(rr_a[:], s2[:, 0:C]).then_inc(a_x1n, 1)
                dve.wait_ge(a_x1n, count(i, X1N, db, 1))
                for c in range(C):
                    dve.scalar_tensor_tensor(x1n[:, c, :], s0[:, c * D:(c + 1) * D], rr_a[:, c:c + 1], x_in[:, c, :],
                                             ALU.mult, ALU.add).then_inc(a_x1n, 1)

            def low_parts(i, db, g, parts, bank):
                dve.wait_ge(g.hi_s, count(i, 1, db, 1))
                dve.tensor_tensor(parts[:, 1, :], bank[:], parts[:, 0, :], ALU.subtract).then_inc(g.lo_s, 1)

            def top_two(i, db, g, bank, part):
                def after(n):
                    dve.wait_ge(g.top, count(i, TOP, db, n))

                def largest(k, src, n):
                    after(n)
                    dve.tensor_reduce(g.m[:, 2 * k, :], src[:], AX_X, ALU.max).then_inc(g.top, 1)

                def equal(k, src, n):
                    after(n)
                    dve.tensor_tensor(g.q[:, 2 * k], src[:], bcast(g.m[:, 2 * k, :], E), ALU.is_equal).then_inc(g.top, 1)

                def ranked(k, n):
                    after(n)
                    dve.tensor_tensor(g.q[:, 2 * k + 1], g.q[:, 2 * k],
                                      ramp[:].unsqueeze(1).to_broadcast([P, C, E]), ALU.mult).then_inc(g.top, 1)

                def first_of_equal(k, n):
                    after(n)
                    dve.tensor_reduce(g.m[:, 2 * k + 1, :], g.q[:, 2 * k + 1], AX_X, ALU.max).then_inc(g.top, 1)
                    after(n + 1)
                    dve.tensor_tensor(g.one[:, k], g.q[:, 2 * k + 1], bcast(g.m[:, 2 * k + 1, :], E), ALU.is_equal)\
                       .then_inc(g.top, 1)

                if part == 0:
                    logits = bank[:, 0:C * E].rearrange("p (c e) -> p c e", c=C)
                    dve.wait_ge(g.logits, count(i, 1, db, 1))
                    if g is gates[0]:
                        dve.tensor_scalar(g.lg[:], logits, 1.0 / WSCALE, None, ALU.mult).then_inc(g.top, 1)
                    else:
                        dve.scalar_tensor_tensor(g.lg[:], logits, 1.0 / WSCALE,
                                                 bg_b[:].unsqueeze(1).to_broadcast([P, C, E]), ALU.mult,
                                                 ALU.add).then_inc(g.top, 1)
                    largest(0, g.lg, 1)
                    equal(0, g.lg, 2)
                    ranked(0, 3)
                if part == 1:
                    first_of_equal(0, 4)
                    after(6)
                    dve.scalar_tensor_tensor(g.lg2[:], g.one[:, 0], NOT_AGAIN, g.lg[:], ALU.mult, ALU.add)\
                       .then_inc(g.top, 1)
                    largest(1, g.lg2, 7)
                if part == 2:
                    equal(1, g.lg2, 8)
                    ranked(1, 9)
                    first_of_equal(1, 10)
                    dve.tensor_tensor(g.m[:, 4, :], g.m[:, 2, :], g.m[:, 0, :], ALU.subtract).then_inc(g.top, 1)

            def masks(i, db, g):
                if g is gates[0]:
                    dve.wait_ge(g.tanh, count(i, 1, db, 1))
                    dve.tensor_scalar(g.w[:, 0, :], g.th[:], -0.5, 0.5, ALU.mult, ALU.add).then_inc(g.mask_d, 1)
                    dve.tensor_scalar(g.w[:, 1, :], g.th[:], 0.5, 0.5, ALU.mult, ALU.add).then_inc(g.mask_d, 1)
                    dve.wait_ge(g.mask_d, count(i, 5, db, 2))
                    for k in range(TOPS):
                        dve.tensor_tensor(g.q[:, k], g.one[:, k], bcast(g.w[:, k, :], E), ALU.mult)\
                           .then_inc(g.mask_d, 1)
                    dve.wait_ge(g.mask_d, count(i, 5, db, 4))
                    a, b = g.q[:, 0], g.q[:, 1]
                else:
                    a, b = g.one[:, 0], g.one[:, 1]
                    dve.wait_ge(g.top, count(i, TOP, db, TOP))
                dve.tensor_tensor(g.mask[:].rearrange("p e c -> p c e"), a, b, ALU.add).then_inc(g.mask_d, 1)

            def unit_out(i, u, back=0):
                g = gates[0] if u < A_UNITS else gates[1]
                dve.wait_ge(down, chunks(i, LAST[u] + 1, back))
                y = ps_y[u % 2]
                if u == 0:
                    dve.tensor_scalar(g.acc[:], y[:], b2x[:, 0:1], 1.0 / WSCALE, ALU.add, ALU.mult).then_inc(evac, 1)
                    return
                e = (u - 1) % E
                if e % 2 == 0:
                    dve.wait_ge(g.mb_in[e // 2], count(i, 16, 0 if u < A_UNITS else -1 - back, 16))
                dst = g.acc if u == A_UNITS else scaled
                if dst is scaled:
                    need(dve, summed, sums(i, u, back))
                dve.scalar_tensor_tensor(dst[:], y[:], b2x[:, u:u + 1], g.mb[:, e, :], ALU.add, ALU.mult)\
                   .then_inc(evac, 1)

            def finish(i, db):
                dve.wait_ge(gates[1].acc_tr, count(i, 1, db, 1))
                need(dve, stored, count(i, 16, db, 0))
                dve.tensor_tensor(x4[:], s0[:].rearrange("p (c d) -> p c d", c=C), x3[:], ALU.add)\
                   .then_inc(x4_made, 1)

            def iteration(i):
                experts0, layer1, next0, last1 = has(i)
                for s in range(SLOTS):
                    if isinstance(i, int) and i == -1 and s == 0:
                        setup()
                    if layer1:
                        if s == DVE_AT["f_b"]:
                            dve.wait_ge(b_f, count(i, 1, -1, 1))
                            dve.wait_ge(b_norm, count(i, 2, -1, 2))
                            dve.tensor_tensor(f_b[:], s1[:].rearrange("p (c d) -> p c d", c=C),
                                              bcast(dg_b[:, 2, :], D), ALU.mult).then_inc(b_fn, 1)
                        if s == DVE_AT["mix_1"]:
                            dve.wait_ge(b_hets, count(i, 1, -1, 1))
                            dve.wait_ge(b_hom, count(i, 1, -1, 1))
                            dve.tensor_tensor(d_b[:], s2[:], het_b[:], ALU.subtract).then_inc(b_mix, 1)
                            dve.wait_ge(b_tanh, count(i, 1, -1, 1))
                            dve.wait_ge(b_mix, count(i, MIX, -1, 1))
                            dve.scalar_tensor_tensor(d_b[:], tg_b[:], 1.0, d_b[:], ALU.add, ALU.mult).then_inc(b_mix, 1)
                        if s == DVE_AT["mix_2"]:
                            dve.wait_ge(b_mix, count(i, MIX, -1, 2))
                            dve.scalar_tensor_tensor(o_b[:], d_b[:], 0.5, het_b[:], ALU.mult, ALU.add).then_inc(b_mix, 1)
                        if s == DVE_AT["mix_3"]:
                            dve.wait_ge(b_mix, count(i, MIX, -1, 3))
                            dve.tensor_scalar(d_b[:], o_b[:], 0.0, None, ALU.min).then_inc(b_mix, 1)
                        if s == DVE_AT["elu"]:
                            dve.wait_ge(b_exp, count(i, 1, -1, 1))
                            dve.scalar_tensor_tensor(o_b[:], o_b[:], 0.0, d_b[:], ALU.max, ALU.add).then_inc(b_elu, 1)
                        if s == DVE_AT["x3"]:
                            dve.wait_ge(b_otr, count(i, 1, -1, 1))
                            dve.scalar_tensor_tensor(x3[:], s1[:].rearrange("p (c d) -> p c d", c=C), -1.0, x2[:],
                                                     ALU.add, ALU.add).then_inc(x3_made, 1)
                        if s == DVE_AT["stats_1"]:
                            dve.wait_ge(x3_made, count(i, 1, -1, 1))
                            stats(i, -1, x3, gates[1].st, gates[1].mv, gates[1].stats)
                        if s == DVE_AT["norm_1"]:
                            normed(i, -1, gates[1].xn, x3, gates[1].mv, gates[1].rs, gates[1].rstd, gates[1].xn_s)
                        if s == DVE_AT["low_1"]:
                            low_parts(i, -1, gates[1], gates[1].xt, s1)
                        if s in DVE_AT["top_1"]:
                            top_two(i, -1, gates[1], s2, DVE_AT["top_1"].index(s))
                        if s == DVE_AT["masks_1"]:
                            masks(i, -1, gates[1])
                    if next0:
                        if s == DVE_AT["stats_a"]:
                            dve.wait_ge(x_landed, count(i, 16, 1, 16))
                            stats(i, 1, x_in, st_a, mv_a, a_stats)
                        if s == DVE_AT["norm_a"]:
                            normed(i, 1, xn_a, x_in, mv_a, rs_a, a_rstd, a_xn)
                        if s in DVE_AT["softmax"]:
                            softmax_logits(i, 1, DVE_AT["softmax"].index(s))
                        if s == DVE_AT["numerators"]:
                            softmax_numerators(i, 1)
                        if s == DVE_AT["attend"]:
                            add_attention(i, 1)
                        if s == DVE_AT["stats_0"]:
                            dve.wait_ge(a_x1n, count(i, X1N, 1, X1N))
                            stats(i, 1, x1n, gates[0].st, gates[0].mv, gates[0].stats)
                        if s == DVE_AT["norm_0"]:
                            normed(i, 1, gates[0].xn, x1n, gates[0].mv, gates[0].rs, gates[0].rstd, gates[0].xn_s)
                        if s == DVE_AT["low_0"]:
                            low_parts(i, 1, gates[0], gates[0].next, s0)
                        if s in DVE_AT["top_0"]:
                            top_two(i, 1, gates[0], s1, DVE_AT["top_0"].index(s))
                        if s == DVE_AT["move_0"]:
                            dve.wait_ge(gates[0].lo_s, count(i, 1, 1, 1))
                            if experts0:
                                dve.wait_ge(up, chunks(i, A_SLOTS))
                            dve.tensor_copy(gates[0].xt[:], gates[0].next[:]).then_inc(gates[0].moved, 1)
                        if s == DVE_AT["masks_0"]:
                            masks(i, 1, gates[0])
                    if s == DVE_AT["x2"]:
                        if experts0:
                            dve.wait_ge(gates[0].acc_tr, count(i, 1, 0, 1))
                            dve.tensor_tensor(x2[:], s2[:].rearrange("p (c d) -> p c d", c=C), x1[:], ALU.add)\
                               .then_inc(x2_made, 1)
                            dve.wait_ge(x2_made, count(i, 1, 0, 1))
                            stats(i, 0, x2, st_b, mv_b, b_stats)
                    if s == DVE_AT["x1"]:
                        if experts0:
                            dve.wait_ge(adjb_landed, count(i, 16, 0, 16))
                            dve.tensor_reduce(dg_b[:, 0, :], adj_b[:], AX_X, ALU.add).then_inc(b_deg, 1)
                        if next0:
                            if not experts0:
                                dve.wait_ge(a_x1n, count(i, X1N, 1, X1N))
                            dve.tensor_copy(x1[:], x1n[:]).then_inc(x1_made, 1)
                    if experts0 and s == DVE_AT["norm_b"]:
                        normed(i, 0, xn_b, x2, mv_b, rs_b, b_rstd, b_xn)
                    if ((experts0 and s < A_SLOTS) or (layer1 and s >= A_SLOTS)) and s not in WHOLE + BY_POOL:
                        k = s % H_SLOTS
                        dve.wait_ge(gelu, chunks(i, s + 1))
                        dve.tensor_tensor(hlo[k][:], h32[k][:], hhi[k][:], ALU.subtract).then_inc(low, 1)
                    for u in range(UNITS):
                        if LAST[u] + LAG == s and (experts0 if u < A_UNITS else layer1):
                            unit_out(i, u)
                        if LAST[u] + LAG == s + SLOTS and last1:
                            unit_out(i, u, 1)
                    if last1 and s == DVE_AT["x4"]:
                        finish(i, -2)
                    if isinstance(i, int) and i < 1:
                        for n in range(2 * PIECES):
                            if PIECE_AT[n] == (i + 1) * SLOTS + s:
                                weight_piece(n)
                if isinstance(i, int) and i == NB:
                    for u in range(UNITS):
                        if LAST[u] + LAG >= SLOTS:
                            unit_out(i, u)
                    finish(i, -1)

            in_blocks(dve, iteration)

        @block.tensor
        def _(pe):
            def transposes(bank, src):
                for c in range(C):
                    ins = pe.transpose(bank[:, c * P:(c + 1) * P], src[:, c * P:(c + 1) * P], ident[:])
                return ins

            def flat(t):
                return t[:].rearrange("p c d -> p (c d)")

            def setup():
                pe.wait_ge(consts, CONSTS)
                pe.wait_ge(small_in, 16 * SMALL)
                pe.transpose(s1[:, 0:ROWS], rows[:], ident[0:ROWS, 0:ROWS])
                pe.transpose(s2[:, 0:D], gat_w[:], ident[:]).then_inc(setup_pe, 1)
                pe.wait_ge(setup_dve, 3)
                pe.matmul(s2[:, 0:2], gat_wT[:], cols[:, A_ROW:A_ROW + 2], start=True, stop=True).then_inc(setup_pe, 1)

            def up_product(i, s):
                g = gates[0] if s < A_SLOTS else gates[1]
                if s == 0:
                    pe.wait_ge(g.moved, count(i, 1, 0, 1))
                if s == A_SLOTS:
                    pe.wait_ge(g.lo_s, count(i, 1, -1, 1))
                if isinstance(i, int) and i <= 1:
                    pe.wait_ge(w_lo, min(2 * (s // C + 1), 2 * PIECES))
                need(pe, gelu, bank_free(i, s))
                h = ps_h[H_BANK[s]]
                pe.matmul(h[:], w1h[:, s, :], g.xt[:, 0, :], start=True, stop=False)
                pe.matmul(h[:], w1l[:, s, :], g.xt[:, 0, :], start=False, stop=False)
                pe.matmul(h[:], w1h[:, s, :], g.xt[:, 1, :], start=False, stop=True).then_inc(up, 1)

            def down_product(i, s, back=0):
                u = UNIT_OF[s]
                k = s % H_SLOTS
                y = ps_y[u % 2]
                first, last = s == FIRST[u], s == LAST[u]
                if first:
                    need(pe, evac, units(i, 0, back) if u == 0 else units(i, u, back) - 1)
                if s in WHOLE:
                    pe.wait_ge(gelu, chunks(i, s + 1, back))
                    pe.matmul(y[:], w2f[:, WHOLE.index(s), :], h32[k][:], start=first, stop=last).then_inc(down, 1)
                    return
                pool_made = s in BY_POOL
                pe.wait_ge(low_pool if pool_made else low, lows(i, s + 1, pool_made, back))
                pe.matmul(y[:], w2h[:, s, :], hhi[k][:], start=first, stop=False)
                pe.matmul(y[:], w2l[:, s, :], hhi[k][:], start=False, stop=False)
                pe.matmul(y[:], w2h[:, s, :], hlo[k][:], start=False, stop=last).then_inc(down, 1)

            def logits(i, db, g, parts, n, bank):
                pe.wait_ge(g.lo_s, count(i, 1, db, 1))
                for c in range(C):
                    o = bank[:, c * E:(c + 1) * E]
                    t = slice(c * P, (c + 1) * P)
                    pe.matmul(o, parts[:, 0, t], gate_h[:, n, :], start=True, stop=False)
                    pe.matmul(o, parts[:, 0, t], gate_l[:, n, :], start=False, stop=False)
                    ins = pe.matmul(o, parts[:, 1, t], gate_h[:, n, :], start=False, stop=True)
                ins.then_inc(g.logits, 1)

            def mask_transpose(i, db, g, bank):
                pe.wait_ge(g.mask_d, count(i, 5 if g is gates[0] else 1, db, 5 if g is gates[0] else 1))
                pe.transpose(bank[0:E * C, 0:P], g.mask[:].rearrange("p e c -> p (e c)"), ident[:])\
                  .then_inc(g.mask_tr, 1)

            def acc_transpose(i, db):
                pe.wait_ge(summed, sums(i, UNITS, -1 - db))
                transposes(s0, gates[1].acc).then_inc(gates[1].acc_tr, 1)

            def iteration(i):
                experts0, layer1, next0, last1 = has(i)
                if isinstance(i, int) and i == -1:
                    setup()
                for s in range(SLOTS):
                    if layer1:
                        if s == PE_AT["f"]:
                            pe.wait_ge(b_xt, count(i, 1, -1, 1))
                            for c in range(C):
                                ins = pe.matmul(s1[:, c * D:(c + 1) * D], xt_b[:, c * P:(c + 1) * P], theta_w[:],
                                                start=True, stop=True)
                            ins.then_inc(b_f, 1)
                        if s == PE_AT["adj_tr"]:
                            pe.wait_ge(b_adjn, count(i, 2, -1, 2))
                            transposes(s2, flat(an_b)).then_inc(b_atr, 1)
                        if s == PE_AT["gate_b"]:
                            pe.matmul(s0[:], wt_w[:], xt_b[:], start=True, stop=True).then_inc(b_gate, 1)
                        if s == PE_AT["acc1_tr"] and last1:
                            pe.wait_ge(b_tanh, count(i, 1, -1, 1))
                            acc_transpose(i, -2)
                        if s == PE_AT["het"]:
                            pe.wait_ge(b_fn, count(i, 1, -1, 1))
                            pe.matmul(s1[:], wh_w[:], xt_b[:], start=True, stop=True).then_inc(b_het, 1)
                        if s == PE_AT["hom"]:
                            pe.wait_ge(b_at, count(i, 1, -1, 1))
                            for c in range(C):
                                t = slice(c * P, (c + 1) * P)
                                ins = pe.matmul(s2[:, t], f_b[:, c, :], at_b[:, t], start=True, stop=True)
                            ins.then_inc(b_hom, 1)
                        if s == PE_AT["o_tr"]:
                            pe.wait_ge(b_elu, count(i, 1, -1, 1))
                            transposes(s1, o_b).then_inc(b_otr, 1)
                        if s == PE_AT["xn1_tr"]:
                            pe.wait_ge(gates[1].xn_s, count(i, 1, -1, 1))
                            transposes(s1, flat(gates[1].xn)).then_inc(gates[1].tr, 1)
                        if s == PE_AT["logits_1"]:
                            if next0:
                                pe.wait_ge(a_x1n, count(i, X1N, 1, X1N))
                            logits(i, -1, gates[1], gates[1].xt, 1, s2)
                        if s == PE_AT["mask1_tr"]:
                            mask_transpose(i, -1, gates[1], s2)
                    if next0:
                        if s == PE_AT["xa_tr"]:
                            pe.wait_ge(a_xn, count(i, 1, 1, 1))
                            if last1:
                                pe.wait_ge(x4_made, count(i, 1, -2, 1))
                            elif layer1:
                                pe.wait_ge(b_tanh, count(i, 1, -1, 1))
                            transposes(s0, flat(xn_a)).then_inc(a_tr, 1)
                        if s == PE_AT["scores"]:
                            pe.wait_ge(a_xt, count(i, 1, 1, 1))
                            if layer1:
                                pe.wait_ge(b_hets, count(i, 1, -1, 1))
                            if isinstance(i, int) and i == -1:
                                pe.wait_ge(setup_dve, 7)
                            for c in range(C):
                                pe.matmul(s1[:, c:c + 1], xt_a[:, c * P:(c + 1) * P], wa[:, 0:1], start=True, stop=True)
                            pe.matmul(s0[:], wa2_rep[:], xt_a[:], start=True, stop=True).then_inc(a_s, 1)
                        if s == PE_AT["wh"]:
                            if layer1:
                                pe.wait_ge(b_mix, count(i, MIX, -1, 1))
                            for c in range(C):
                                ins = pe.matmul(s2[:, c * D:(c + 1) * D], xt_a[:, c * P:(c + 1) * P], gat_w[:],
                                                start=True, stop=True)
                            ins.then_inc(a_wh, 1)
                        if s == PE_AT["p_tr"]:
                            pe.wait_ge(a_prob, count(i, 1, 1, 1))
                            transposes(s0, flat(pr_a)).then_inc(a_ptr, 1)
                        if s == PE_AT["out"]:
                            pe.wait_ge(a_pt, count(i, 1, 1, 1))
                            pe.wait_ge(a_whs, count(i, 1, 1, 1))
                            for c in range(C):
                                t = slice(c * P, (c + 1) * P)
                                pe.matmul(s2[:, c:c + 1], pt_a[:, t], ones[:, 0:1], start=True, stop=True)
                            for c in range(C):
                                t = slice(c * P, (c + 1) * P)
                                ins = pe.matmul(s0[:, t], pt_a[:, t], wh_a[:, t], start=True, stop=True)
                            ins.then_inc(a_out, 1)
                        if s == PE_AT["xn0_tr"]:
                            pe.wait_ge(gates[0].xn_s, count(i, 1, 1, 1))
                            transposes(s0, flat(gates[0].xn)).then_inc(gates[0].tr, 1)
                        if s == PE_AT["logits_0"]:
                            logits(i, 1, gates[0], gates[0].next, 0, s1)
                        if s == PE_AT["mask0_tr"]:
                            mask_transpose(i, 1, gates[0], s1)
                    if experts0:
                        if s == PE_AT["acc0_tr"]:
                            pe.wait_ge(summed, sums(i, A_UNITS))
                            if layer1:
                                pe.wait_ge(gates[1].mask_row, count(i, 1, -1, 1))
                            transposes(s2, gates[0].acc).then_inc(gates[0].acc_tr, 1)
                        if s == PE_AT["xb_tr"]:
                            pe.wait_ge(b_xn, count(i, 1, 0, 1))
                            if next0:
                                pe.wait_ge(gates[0].mask_row, count(i, 1, 1, 1))
                            transposes(s1, flat(xn_b)).then_inc(b_tr, 1)
                    if (experts0 and s < A_SLOTS) or (layer1 and s >= A_SLOTS):
                        up_product(i, s)
                    t = s - LAG
                    if t >= 0 and ((experts0 and t < A_SLOTS) or (layer1 and t >= A_SLOTS)):
                        down_product(i, t)
                    if t < 0 and last1:
                        down_product(i, t + SLOTS, 1)
                if isinstance(i, int) and i == NB:
                    for t in range(SLOTS - LAG, SLOTS):
                        down_product(i, t)
                    acc_transpose(i, -1)

            in_blocks(pe, iteration)


_NAMES = ["x", "adj", "L0_gnn_W", "L0_gnn_a", "L0_ffn_Wr", "L0_ffn_W1s", "L0_ffn_b1s", "L0_ffn_W2s", "L0_ffn_b2s",
          "L0_ffn_W1p", "L0_ffn_b1p", "L0_ffn_W2p", "L0_ffn_b2p", "L1_gnn_W_t", "L1_gnn_b_t", "L1_gnn_W_h",
          "L1_gnn_theta", "L1_ffn_Wg", "L1_ffn_bg", "L1_ffn_W1", "L1_ffn_b1", "L1_ffn_W2", "L1_ffn_b2"]


def kernel(**inputs):
    import numpy as np
    import concourse.bacc as bacc
    from concourse.bass_utils import run_bass_kernel_spmd

    nc = bacc.Bacc("TRN2", target_bir_lowering=False, num_devices=1)
    arrays, args = {}, []
    for name in _NAMES:
        a = np.ascontiguousarray(inputs[name])
        arrays[f"in_{name}"] = a
        args.append(nc.dram_tensor(f"in_{name}", a.shape, mybir.dt.from_np(a.dtype), kind="ExternalInput").ap())
    args.append(nc.dram_tensor("result", inputs["x"].shape, F32, kind="ExternalOutput").ap())
    mk_adj_ffn_kernel(nc, *args)
    r = run_bass_kernel_spmd(nc, [arrays], core_ids=[0])
    return r.results[0]["result"]
```

```python
from contextlib import ExitStack

import concourse.bass as bass
from concourse import mybir

F32 = mybir.dt.float32
F16 = mybir.dt.float16
ALU = mybir.AluOpType
ACT = mybir.ActivationFunctionType
AX_X = mybir.AxisListType.X

P = 128
D = 128
C = 4
BLK = C * P
E = 8
TOPS = 2
WSCALE = 256.0
ALPHA = 0.2
NOT_AGAIN = -1.0e30

H_SLOTS = 4
LAG = 3
WHOLE = (12, 44)
CAST = (13, 26, 50)
BY_POOL = (7, 17, 24, 41, 42)
PIECE_AT = (
    9, 9, 10, 11, 12, 16, 20, 20, 24, 25, 29, 31, 54,
    57, 57, 59, 62, 64, 66, 67, 67, 69, 69, 73, 73, 75,
)
XB_LATE = 1
TANH_LATE, MASKS_LATE, MASK_TR_LATE, ROWS_LATE = 1, 1, 4, 4
SETUP_AT = 9
PE_AT = {
    "adj_tr": 2, "f": 3, "gate_b": 3, "acc1_tr": 6, "het": 7, "hom": 7, "xa_tr": 9, "scores": 11, "wh": 11,
    "o_tr": 16, "p_tr": 17, "out": 22, "xn1_tr": 26, "logits_1": 30, "xn0_tr": 32, "logits_0": 37, "mask1_tr": 38,
    "acc0_tr": 43, "mask0_tr": 45, "xb_tr": 48,
}
ACT_AT = {
    "at_b": 3, "tanh_b": 4, "het_copy": 8, "xt_a": 8, "wh_copy": 11, "exp_b": 14, "exp_a": 14, "pt_copy": 20,
    "hi_1": 25, "hi_0": 32, "rows_1": 38, "tanh_0": 41, "rows_0": 45, "xt_b": 48,
}
DVE_AT = {
    "stats_a": 0, "f_b": 3, "x4": 3, "norm_a": 5, "mix_1": 8, "mix_2": 8, "softmax": (10, 11), "mix_3": 12,
    "elu": 13, "numerators": 14, "sums": 16, "x3": 17, "stats_1": 19, "norm_1": 21, "attend": 24, "stats_0": 24,
    "low_1": 25, "norm_0": 29, "top_1": (30, 31, 32), "low_0": 33, "masks_1": 35, "top_0": (36, 38, 39),
    "move_0": 40, "masks_0": 40, "x2": 43, "x1": 45, "norm_b": 45, "low_b": 51,
}
POOL_AT = {
    "rstd_a": 0, "s1": 6, "rstd_1": 22, "rstd_0": 25, "rstd_b": 44, "adj_norm": 45,
}


def mk_adj_ffn_kernel(
    nc, x, adj, gat_W, gat_a, Wr, W1s, b1s, W2s, b2s, W1p, b1p, W2p, b2p,
    W_t, b_t, W_h, theta, Wg, bg, W1, b1, W2, b2, out,
):
    graphs, nodes, _ = x.shape
    gpt = P // nodes
    NB = graphs * nodes // BLK
    SH = W1s.shape[1] // P
    K0 = W1p.shape[2] // P
    K1 = W1.shape[2] // P
    A_SLOTS = SH + E * K0
    SLOTS = A_SLOTS + E * K1
    UNIT_LEN = [SH] + [K0] * E + [K1] * E
    UNITS = len(UNIT_LEN)
    A_UNITS = 1 + E
    UNIT_OF = [u for u, k in enumerate(UNIT_LEN) for _ in range(k)]
    FIRST = [sum(UNIT_LEN[:u]) for u in range(UNITS)]
    LAST = [sum(UNIT_LEN[:u + 1]) - 1 for u in range(UNITS)]
    assert gpt == 2 and A_SLOTS % H_SLOTS == 0 and SLOTS % H_SLOTS == 0 and SH == K0

    def count(i, per_block, db, n):
        return per_block * i + (per_block * db + n)

    def before(i, n, in_layer0, in_all, back=0):
        if isinstance(i, int):
            i, back = i - back, 0
            if i == 0:
                return n
            if i == NB:
                n -= in_layer0
        return in_all * i + (in_layer0 - in_all + n - in_all * back)

    def chunks(i, s, back=0):
        return before(i, s, A_SLOTS, SLOTS, back)

    BY_DVE = [s for s in range(SLOTS) if s not in WHOLE + BY_POOL]

    def those(i, s, some, back=0):
        def n(end):
            return sum(c < end for c in some)

        return before(i, n(s), n(A_SLOTS), n(SLOTS), back)

    def units(i, u, back=0):
        return before(i, u, A_UNITS, UNITS, back)

    def sums(i, u, back=0):
        return before(i, max(u - 1, 0) - (1 if u > A_UNITS else 0), E, 2 * E - 1, back)

    H_BANK = [s % 3 for s in range(SLOTS - 1)] + [1]

    def bank_free(i, s):
        near = s in (1, SLOTS - 1) or (isinstance(i, int) and i == NB)
        return chunks(i, s) - (1 if near else 2)

    def need(eng, sem, value):
        if not isinstance(value, int) or value > 0:
            eng.wait_ge(sem, value)

    def in_blocks(eng, body, last=2):
        body(-1)
        body(0)
        body(1)
        with eng.Fori(2, NB + 1 - last) as i:
            body(i)
        for i in range(NB + 1 - last, NB + 1):
            body(i)

    def has(i):
        if not isinstance(i, int):
            return True, True, True, True
        return 0 <= i < NB, 1 <= i <= NB, i + 1 < NB, 2 <= i <= NB

    def is_first(i):
        return isinstance(i, int) and i == 0

    def is_fill(i):
        return isinstance(i, int) and i == -1

    x_v = x.rearrange("(b c g) n d -> b (g n) c d", c=C, g=gpt)
    out_v = out.rearrange("(b c g) n d -> b (g n) c d", c=C, g=gpt)
    adj_v = adj.rearrange("(b c g) n m -> b (g n) c m", c=C, g=gpt)

    def block_of(view, b):
        return view[b] if isinstance(b, int) else view[bass.ds(b, 1)].rearrange("b p c d -> (b p) c d")

    with ExitStack() as ctx:
        def sb(name, shape, dt=F32):
            return ctx.enter_context(nc.sbuf_tensor(name, shape, dt))

        def sem(name):
            return ctx.enter_context(nc.semaphore(name))

        ps_h = [ctx.enter_context(nc.psum_tensor(f"ps_h{k}", [P, BLK], F32)) for k in range(3)]
        ps_y = [ctx.enter_context(nc.psum_tensor(f"ps_y{k}", [P, BLK], F32)) for k in range(2)]
        s0, s1, s2 = (ctx.enter_context(nc.psum_tensor(f"ps_s{k}", [P, BLK], F32)) for k in range(3))

        w1h = sb("w1h", [P, SLOTS, P], F16)
        w1l = sb("w1l", [P, SLOTS, P], F16)
        w2h = sb("w2h", [P, SLOTS, P], F16)
        w2l = sb("w2l", [P, SLOTS, P], F16)
        w2f = sb("w2f", [P, len(WHOLE), P])
        PIECES = SLOTS // C
        STAGES = 8
        stage = [sb(f"stage{k}", [P, C, P]) for k in range(STAGES)]
        gat_w = sb("gat_w", [P, D])
        THETA, WH, WT = range(3)
        gcn_f = sb("gcn_f", [P, 3, D])
        gcn_h = sb("gcn_h", [P, 3, D], F16)
        gcn_l = sb("gcn_l", [P, 3, D], F16)
        gate_f = sb("gate_f", [P, 2, E])
        gate_h = sb("gate_h", [P, 2, E], F16)
        gate_l = sb("gate_l", [P, 2, E], F16)
        ROWS = SLOTS + UNITS + 3
        A_ROW = SLOTS + UNITS
        rows = sb("rows", [ROWS, P])
        cols = sb("cols", [P, ROWS])
        b2x = sb("b2x", [P, UNITS])
        bt_half = sb("bt_half", [P, 1])
        gat_wT = sb("gat_wT", [P, D])
        a1_rep = sb("a1_rep", [P, P])
        wa1_row = sb("wa1_row", [P, D])
        wa2 = sb("wa2", [P, 1])
        wa2_rep = sb("wa2_rep", [P, P])
        bg_b = sb("bg_b", [P, E])
        ident = sb("ident", [P, P])
        ramp = sb("ramp", [P, E])
        neg_half = sb("neg_half", [P, C])
        carrier = sb("carrier", [P, 1])
        eps = sb("eps", [P, 2, C])

        x_in = sb("x_in", [P, C, D])
        adj_a = sb("adj_a", [P, C, nodes])
        st_a = sb("st_a", [P, C, 6])
        mv_a = sb("mv_a", [P, C, 2])
        rs_a = sb("rs_a", [P, 2, C])
        xn_a = sb("xn_a", [P, C, D])
        xt_a = sb("xt_a", [P, BLK])
        s1p = sb("s1p", [P, C, D])
        row_sum = sb("row_sum", [P, C])
        s1c = sb("s1c", [P, 4, C])
        u_a = sb("u_a", [P, C, nodes])
        e_a = sb("e_a", [P, C, nodes])
        pr_a = sb("pr_a", [P, C, P])
        pt_a = sb("pt_a", [P, BLK])
        wh_a = sb("wh_a", [P, BLK])
        rr_a = sb("rr_a", [P, C])
        x1n = sb("x1n", [P, C, D])
        x1 = sb("x1", [P, C, D])
        adj_b = sb("adj_b", [P, C, nodes])
        st_b = sb("st_b", [P, C, 6])
        mv_b = sb("mv_b", [P, C, 2])
        rs_b = sb("rs_b", [P, 2, C])
        dg_b = sb("dg_b", [P, 3, C])
        an_b = sb("an_b", [P, C, P])
        at_b = sb("at_b", [P, BLK])
        xn_b = sb("xn_b", [P, C, D])
        xt_b = sb("xt_b", [P, 2, BLK], F16)
        f_b = sb("f_b", [P, C, D])
        tg_b = sb("tg_b", [P, BLK])
        het_b = sb("het_b", [P, BLK])
        d_b = sb("d_b", [P, BLK])
        o_b = sb("o_b", [P, BLK])
        x2 = sb("x2", [P, C, D])
        x3 = sb("x3", [P, C, D])
        x4 = sb("x4", [P, C, D])

        class Gate:
            def __init__(self, n):
                self.st = sb(f"st_f{n}", [P, C, 6])
                self.mv = sb(f"mv_f{n}", [P, C, 2])
                self.rs = sb(f"rs_f{n}", [P, 2, C])
                self.xn = sb(f"xn_f{n}", [P, C, D])
                self.xt = sb(f"xt{n}", [P, 2, BLK], F16)
                if n == 0:
                    self.next = sb("xt_next", [P, 2, BLK], F16)
                self.lg = sb(f"lg{n}", [P, C, E])
                self.lg2 = sb(f"lg2{n}", [P, C, E])
                self.q = sb(f"q{n}", [P, 4, C, E])
                self.one = sb(f"one{n}", [P, 2, C, E])
                self.m = sb(f"m{n}", [P, 5, C])
                self.th = sb(f"th{n}", [P, C])
                self.w = sb(f"w{n}", [P, 2, C])
                self.mask = sb(f"mask{n}", [P, E, C])
                self.mt = sb(f"mt{n}", [E * C, P])
                self.mb = sb(f"mb{n}", [P, E, BLK])
                self.dram = nc.dram_tensor(f"mask_rows{n}", (E * C, P), F32, kind="Internal").ap()
                self.acc = sb(f"acc{n}", [P, BLK])
                self.stats, self.rstd, self.xn_s, self.tr, self.hi_s, self.lo_s, self.logits = (
                    sem(f"{s}{n}") for s in ("stats", "rstd", "xn", "tr", "hi", "lo", "logits"))
                self.top, self.tanh, self.mask_d, self.mask_tr, self.mask_row, self.acc_tr = (
                    sem(f"{s}{n}") for s in ("top", "tanh", "mask_d", "mask_tr", "mask_row", "acc_tr"))
                self.moved = sem(f"moved{n}")
                self.row_out = sem(f"mask_out{n}")
                self.mb_in = [sem(f"mask_in{n}_{k}") for k in range(E // 2)]

        gates = [Gate(0), Gate(1)]
        scaled = sb("scaled", [P, BLK])
        h32 = [sb(f"h32_{k}", [P, BLK]) for k in range(H_SLOTS)]
        hhi = [sb(f"hhi_{k}", [P, BLK], F16) for k in range(H_SLOTS)]
        hlo = [sb(f"hlo_{k}", [P, BLK], F16) for k in range(H_SLOTS)]

        small_in = sem("small_in")
        layer1_in = sem("layer1_in")
        stage_in = [sem(f"stage_in{k}") for k in range(STAGES)]
        w_hi = sem("w_hi")
        w_lo = sem("w_lo")
        consts = sem("consts")
        zeroed = sem("zeroed")
        setup_pe = sem("setup_pe")
        setup_dve = sem("setup_dve")
        gate_hi = sem("gate_hi")

        x_landed, adja_landed, adjb_landed, stored = sem("x_landed"), sem("adja_landed"), sem("adjb_landed"), sem("stored")
        gcn_hi, gcn_lo, b_xlo = sem("gcn_hi"), sem("gcn_lo"), sem("b_xlo")
        a_stats, a_rstd, a_xn, a_tr, a_xt = (sem(n) for n in ("a_stats", "a_rstd", "a_xn", "a_tr", "a_xt"))
        a_s1p, a_sum = sem("a_s1p"), sem("a_sum")
        a_s, a_soft, a_exp, a_prob, a_ptr, a_pt, a_wh, a_whs, a_out, a_x1n, x1_made = (sem(n) for n in (
            "a_s", "a_soft", "a_exp", "a_prob", "a_ptr", "a_pt", "a_wh", "a_whs", "a_out", "a_x1n", "x1_made"))
        b_stats, b_rstd, b_xn, b_tr, b_xt, b_deg, b_norm, b_adjn = (sem(n) for n in (
            "b_stats", "b_rstd", "b_xn", "b_tr", "b_xt", "b_deg", "b_norm", "b_adjn"))
        b_f, b_fn, b_atr, b_at, b_gate, b_tanh, b_het, b_hets, b_hom, b_mix, b_exp, b_elu, b_otr, x3_made = (
            sem(n) for n in ("b_f", "b_fn", "b_atr", "b_at", "b_gate", "b_tanh", "b_het", "b_hets", "b_hom",
                             "b_mix", "b_exp", "b_elu", "b_otr", "x3_made"))
        x2_made, x4_made = sem("x2_made"), sem("x4_made")
        up = sem("up")
        gelu = sem("gelu")
        low = sem("low")
        low_pool = sem("low_pool")
        cast = sem("cast")
        down = sem("down")
        evac = sem("evac")
        summed = sem("summed")
        SMALL = 11
        CONSTS = 6 + E

        STATS, SOFT, TOP, X1N, MIX = 2 * C, 8, 13, C + 1, 4

        def bcast(ap, n):
            return ap.unsqueeze(2).to_broadcast([ap.shape[0], ap.shape[1], n])

        block = ctx.enter_context(nc.Block())

        @block.sync
        def _(sp):
            def load(i, db):
                src_x, src_a = block_of(x_v, i + db), block_of(adj_v, i + db)
                need(sp, a_x1n, count(i, X1N, db, 0))
                sp.dma_start(x_in[:], src_x).then_inc(x_landed, 16)
                sp.dma_start(adj_a[:], src_a).then_inc(adja_landed, 16)

            load(-1, 1)
            for dst, src in (
                (gat_w[:], gat_W), (gate_f[:, 0], Wr), (gate_f[:, 1], Wg),
                (rows[0:SH], b1s.rearrange("(k p) -> k p", p=P)),
                (rows[SH:A_SLOTS], b1p.rearrange("e (k p) -> (e k) p", p=P)),
                (rows[A_SLOTS:SLOTS], b1.rearrange("e (k p) -> (e k) p", p=P)),
                (rows[SLOTS:SLOTS + 1], b2s.rearrange("(k p) -> k p", p=P)),
                (rows[SLOTS + 1:SLOTS + 1 + E], b2p), (rows[SLOTS + 1 + E:SLOTS + UNITS], b2),
                (rows[A_ROW:A_ROW + 2], gat_a.rearrange("(k p) u -> k (p u)", p=P)),
                (rows[A_ROW + 2:A_ROW + 3], b_t.rearrange("(k p) -> k p", p=P)),
            ):
                sp.dma_start(dst, src).then_inc(small_in, 16)

            def weight_pieces(some):
                for n in some:
                    p, second = n // 2, n % 2
                    if n >= STAGES:
                        sp.wait_ge(w_lo, n - STAGES + 1)
                    if p == 0:
                        src = W2s.rearrange("(k p) d -> p k d", p=P) if second else W1s.rearrange("d (k p) -> d k p", p=P)
                        sp.dma_start(stage[n % STAGES][:], src).then_inc(stage_in[n % STAGES], 16)
                    elif p <= E:
                        src = (W2p[p - 1].rearrange("(k p) d -> p k d", p=P) if second
                               else W1p[p - 1].rearrange("d (k p) -> d k p", p=P))
                        sp.dma_start(stage[n % STAGES][:], src).then_inc(stage_in[n % STAGES], 16)
                    else:
                        e = (p - 1 - E) * (C // K1)
                        for j in range(C // K1):
                            src = (W2[e + j].rearrange("(k p) d -> p k d", p=P) if second
                                   else W1[e + j].rearrange("d (k p) -> d k p", p=P))
                            sp.dma_start(stage[n % STAGES][:, j * K1:(j + 1) * K1], src)\
                              .then_inc(stage_in[n % STAGES], 16)

            def masks_out(i, db, g):
                sp.wait_ge(g.mask_row, count(i, 1, db, 1))
                sp.dma_start(g.dram, g.mt[:]).then_inc(g.row_out, 16)
                sp.wait_ge(g.row_out, count(i, 16, db, 16))
                for k in range(E // 2):
                    src = g.dram[2 * k * C:2 * (k + 1) * C].rearrange("(u r) p -> u (r p)", u=1)
                    sp.dma_start(g.mb[:, 2 * k:2 * k + 2, :].rearrange("p e t -> p (e t)"),
                                 src.to_broadcast([P, 2 * BLK])).then_inc(g.mb_in[k], 16)

            def iteration(i):
                experts0, layer1, next0, last1 = has(i)
                if experts0:
                    src_b = block_of(adj_v, i)
                    need(sp, b_adjn, count(i, 2, 0, 0))
                    sp.dma_start(adj_b[:], src_b).then_inc(adjb_landed, 16)
                if last1:
                    store(i, -2)
                early = min(sum(slot < SLOTS for slot in PIECE_AT) + STAGES, 2 * PIECES)
                if isinstance(i, int) and i == -1:
                    weight_pieces(range(early))
                    for dst, src in (
                        (gcn_f[:, THETA], theta), (gcn_f[:, WH], W_h), (gcn_f[:, WT], W_t),
                        (bg_b[:], bg.rearrange("(u e) -> u e", u=1).to_broadcast([P, E])),
                    ):
                        sp.dma_start(dst, src).then_inc(layer1_in, 16)
                if isinstance(i, int) and i == 0:
                    weight_pieces(range(early, 2 * PIECES))
                if layer1:
                    masks_out(i, -1, gates[1])
                if not isinstance(i, int) or i + 2 < NB:
                    load(i, 2)
                if next0:
                    masks_out(i, 1, gates[0])

            def store(i, db):
                dst = block_of(out_v, i + db)
                sp.wait_ge(x4_made, count(i, 1, db, 1))
                sp.dma_start(dst, x4[:]).then_inc(stored, 16)

            in_blocks(sp, iteration, 3)
            store(NB, -1)
            sp.wait_ge(stored, 16 * NB)

        @block.gpsimd
        def _(pool):
            pool.memset(ident[:], 0.0).then_inc(consts, 1)
            pool.memset(neg_half[:], -0.5).then_inc(consts, 1)
            pool.memset(eps[:, 0, :], 1.0e-5).then_inc(consts, 1)
            pool.memset(eps[:, 1, :], 1.0e-6).then_inc(consts, 1)
            for e in range(E):
                pool.memset(ramp[:, e:e + 1], float(E - e)).then_inc(consts, 1)
            pool.memset(an_b[:], 0.0).then_inc(consts, 1)
            pool.wait_ge(consts, 1)
            pool.affine_select(out=ident[:], in_=ident[:], compare_op=ALU.not_equal, fill=1.0,
                               base=0, pattern=[[-1, P]], channel_multiplier=1).then_inc(consts, 1)
            pool.wait_ge(consts, CONSTS)

            def rstd(i, db, mv, rs, stats, done):
                pool.wait_ge(stats, count(i, STATS, db, STATS))
                pool.tensor_tensor(rs[:, 0, :], mv[:, :, 1], eps[:, 0, :], ALU.add).then_inc(done, 1)
                pool.wait_ge(done, count(i, 2, db, 1))
                pool.tensor_tensor(rs[:, 1, :], rs[:, 0, :], neg_half[:], ALU.pow).then_inc(done, 1)

            def adj_norm(i, db):
                pool.wait_ge(b_deg, count(i, 1, db, 1))
                pool.tensor_tensor(dg_b[:, 1, :], dg_b[:, 0, :], eps[:, 1, :], ALU.add).then_inc(b_norm, 1)
                pool.wait_ge(b_norm, count(i, 2, db, 1))
                pool.tensor_tensor(dg_b[:, 2, :], dg_b[:, 1, :], neg_half[:], ALU.pow).then_inc(b_norm, 1)
                pool.wait_ge(b_norm, count(i, 2, db, 2))
                need(pool, b_at, count(i, 1, db, 0))
                for h in range(gpt):
                    ps = slice(h * nodes, (h + 1) * nodes)
                    pool.tensor_tensor(an_b[ps, :, ps], adj_b[ps, :, :], bcast(dg_b[ps, 2, :], nodes),
                                       ALU.mult).then_inc(b_adjn, 1)
                    pool.wait_ge(b_adjn, count(i, 2, db, h + 1))

            def unit_add(i, u, back=0):
                if u == 0 or u == A_UNITS:
                    return
                g = gates[0] if u < A_UNITS else gates[1]
                pool.wait_ge(evac, units(i, u + 1, back))
                pool.tensor_tensor(g.acc[:], g.acc[:], scaled[:], ALU.add).then_inc(summed, 1)

            def iteration(i):
                experts0, layer1, next0, last1 = has(i)
                for s in range(SLOTS):
                    if next0 and s == POOL_AT["rstd_a"]:
                        rstd(i, 1, mv_a, rs_a, a_stats, a_rstd)
                    if next0 and s == POOL_AT["s1"]:
                        pool.wait_ge(a_xn, count(i, 1, 1, 1))
                        if isinstance(i, int) and i == -1:
                            pool.wait_ge(setup_dve, 7)
                        pool.tensor_tensor(s1p[:], xn_a[:], wa1_row[:].unsqueeze(1).to_broadcast([P, C, D]),
                                           ALU.mult).then_inc(a_s1p, 1)
                    if layer1 and s == POOL_AT["rstd_1"]:
                        rstd(i, -1, gates[1].mv, gates[1].rs, gates[1].stats, gates[1].rstd)
                    if next0 and s == POOL_AT["rstd_0"]:
                        rstd(i, 1, gates[0].mv, gates[0].rs, gates[0].stats, gates[0].rstd)
                    if experts0 and s == POOL_AT["rstd_b"]:
                        rstd(i, 0, mv_b, rs_b, b_stats, b_rstd)
                    if experts0 and s == POOL_AT["adj_norm"]:
                        adj_norm(i, 0)
                    if ((experts0 and s < A_SLOTS) or (layer1 and s >= A_SLOTS)) and s in BY_POOL:
                        k = s % H_SLOTS
                        if s in CAST:
                            pool.wait_ge(cast, those(i, s + 1, CAST))
                        else:
                            pool.wait_ge(gelu, chunks(i, s + 1))
                        pool.tensor_tensor(hlo[k][:], h32[k][:], hhi[k][:], ALU.subtract).then_inc(low_pool, 1)
                    for u in range(UNITS):
                        if LAST[u] + LAG == s and (experts0 if u < A_UNITS else layer1):
                            unit_add(i, u)
                        if LAST[u] + LAG == s + SLOTS and last1:
                            unit_add(i, u, 1)
                if isinstance(i, int) and i == NB:
                    for u in range(UNITS):
                        if LAST[u] + LAG >= SLOTS:
                            unit_add(i, u)

            in_blocks(pool, iteration)

        @block.scalar
        def _(act):
            def weight_piece(n):
                p = n // 2
                hi = (w2h if n % 2 else w1h)[:, C * p:C * p + C, :]
                halves = 1 if p <= E else C // K1
                before = sum(16 * (1 if m // 2 <= E else C // K1) for m in range(n % STAGES, n, STAGES))
                act.wait_ge(stage_in[n % STAGES], before + 16 * halves)
                act.activation(hi, stage[n % STAGES][:], ACT.Copy, scale=WSCALE).then_inc(w_hi, 1)

            def setup():
                act.wait_ge(small_in, 16 * SMALL)
                act.activation(gate_h[:], gate_f[:], ACT.Copy, scale=WSCALE).then_inc(gate_hi, 1)

            def copy_out(i, db, dst, src, ready, done, scale=1.0):
                act.wait_ge(ready, count(i, 1, db, 1))
                act.activation(dst, src, ACT.Copy, scale=scale).then_inc(done, 1)

            def gate_tanh(i, db, g):
                act.wait_ge(g.top, count(i, TOP, db, TOP))
                act.activation(g.th[:], g.m[:, 4, :], ACT.Tanh, scale=0.5).then_inc(g.tanh, 1)

            def mask_rows(i, db, g, units_before):
                need(act, evac, units_before)
                act.wait_ge(g.mask_tr, count(i, 1, db, 1))
                need(act, g.row_out, count(i, 16, db, 0))
                act.activation(g.mt[:], (s1 if g is gates[0] else s2)[0:E * C, 0:P], ACT.Copy,
                               scale=1.0 / WSCALE).then_inc(g.mask_row, 1)

            def iteration(i):
                experts0, layer1, next0, last1 = has(i)
                for s in range(SLOTS):
                    if layer1:
                        if s == 0 and isinstance(i, int) and i == 1:
                            act.wait_ge(layer1_in, 16 * 4)
                            act.activation(gcn_h[:], gcn_f[:], ACT.Copy, scale=WSCALE).then_inc(gcn_hi, 1)
                        if s == ACT_AT["at_b"]:
                            copy_out(i, -1, at_b[:], s2[:], b_atr, b_at)
                        if s == ACT_AT["tanh_b"]:
                            act.wait_ge(b_gate, count(i, 1, -1, 1))
                            act.activation(tg_b[:], s0[:], ACT.Tanh, bias=bt_half[:, 0:1], scale=0.5 / WSCALE)\
                               .then_inc(b_tanh, 1)
                        if s == ACT_AT["het_copy"]:
                            copy_out(i, -1, het_b[:], s1[:], b_het, b_hets, 1.0 / WSCALE)
                        if s == ACT_AT["exp_b"]:
                            act.wait_ge(b_mix, count(i, MIX, -1, MIX))
                            act.activation(d_b[:], d_b[:], ACT.Exp).then_inc(b_exp, 1)
                        if s == ACT_AT["hi_1"]:
                            copy_out(i, -1, gates[1].xt[:, 0, :], s1[:], gates[1].tr, gates[1].hi_s)
                        if s == ACT_AT["rows_1"]:
                            mask_rows(i, -1, gates[1], units(i, 0) if experts0 else units(i, A_UNITS))
                    if next0:
                        if s == ACT_AT["xt_a"]:
                            copy_out(i, 1, xt_a[:], s0[:], a_tr, a_xt)
                        if s == ACT_AT["wh_copy"]:
                            copy_out(i, 1, wh_a[:], s2[:], a_wh, a_whs)
                        if s == ACT_AT["exp_a"]:
                            act.wait_ge(a_soft, count(i, SOFT, 1, SOFT))
                            act.activation(e_a[:], u_a[:], ACT.Exp).then_inc(a_exp, 1)
                        if s == ACT_AT["pt_copy"]:
                            copy_out(i, 1, pt_a[:], s0[:], a_ptr, a_pt)
                        if s == ACT_AT["hi_0"]:
                            copy_out(i, 1, gates[0].next[:, 0, :], s0[:], gates[0].tr, gates[0].hi_s)
                        if s == ACT_AT["tanh_0"] and not is_fill(i):
                            gate_tanh(i, 1, gates[0])
                        if s == ACT_AT["rows_0"] and not is_fill(i):
                            mask_rows(i, 1, gates[0], units(i, A_UNITS))
                    if is_first(i) and s == TANH_LATE:
                        gate_tanh(i, 0, gates[0])
                    if is_first(i) and s == ROWS_LATE:
                        mask_rows(i, 0, gates[0], 0)
                    if experts0 and s == ACT_AT["xt_b"] and not is_first(i):
                        copy_out(i, 0, xt_b[:, 0, :], s1[:], b_tr, b_xt)
                    if s == XB_LATE and isinstance(i, int) and is_first(i - 1):
                        copy_out(i, -1, xt_b[:, 0, :], s1[:], b_tr, b_xt)
                    if (experts0 and s < A_SLOTS) or (layer1 and s >= A_SLOTS):
                        k = s % H_SLOTS
                        act.wait_ge(up, chunks(i, s + 1))
                        need(act, down, chunks(i, s + 1) - H_SLOTS)
                        ins = act.activation(h32[k][:], ps_h[H_BANK[s]][:], ACT.Gelu, bias=cols[:, s:s + 1],
                                             scale=1.0 / WSCALE)
                        if s not in WHOLE + CAST:
                            ins = act.activation(hhi[k][:], ps_h[H_BANK[s]][:], ACT.Gelu, bias=cols[:, s:s + 1],
                                                 scale=1.0 / WSCALE)
                        ins.then_inc(gelu, 1)
                    if isinstance(i, int) and i < 1:
                        if i == -1 and s == SETUP_AT:
                            setup()
                        for n in range(2 * PIECES):
                            if PIECE_AT[n] == (i + 1) * SLOTS + s:
                                weight_piece(n)

            in_blocks(act, iteration)

        @block.vector
        def _(dve):
            def weight_piece(n):
                p = n // 2
                hi, lo = ((w2h, w2l) if n % 2 else (w1h, w1l))
                dve.wait_ge(w_hi, n + 1)
                for j, w in enumerate(WHOLE):
                    if n % 2 and w // C == p:
                        dve.tensor_scalar(w2f[:, j, :], stage[n % STAGES][:, w % C, :], WSCALE, None, ALU.mult)
                dve.scalar_tensor_tensor(lo[:, C * p:C * p + C, :], stage[n % STAGES][:], WSCALE,
                                         hi[:, C * p:C * p + C, :], ALU.mult, ALU.subtract).then_inc(w_lo, 1)

            def setup():
                dve.memset(pr_a[:], 0.0).then_inc(zeroed, 1)
                dve.wait_ge(zeroed, 1)
                dve.wait_ge(setup_pe, 1)
                dve.tensor_copy(cols[:], s1[:, 0:ROWS]).then_inc(setup_dve, 1)
                dve.tensor_copy(gat_wT[:], s2[:, 0:D]).then_inc(setup_dve, 1)
                dve.wait_ge(setup_dve, 2)
                dve.tensor_copy(a1_rep[:], cols[:, A_ROW:A_ROW + 1].to_broadcast([P, P])).then_inc(setup_dve, 1)
                dve.tensor_scalar(b2x[:], cols[:, SLOTS:SLOTS + UNITS], WSCALE, None, ALU.mult).then_inc(setup_dve, 1)
                dve.tensor_scalar(bt_half[:], cols[:, A_ROW + 2:A_ROW + 3], 0.5, None, ALU.mult).then_inc(setup_dve, 1)
                dve.wait_ge(setup_pe, 2)
                dve.tensor_copy(wa1_row[:], s1[:, 0:D]).then_inc(setup_dve, 1)
                dve.tensor_copy(wa2[:], s2[:, 0:1]).then_inc(setup_dve, 1)
                dve.wait_ge(setup_dve, 7)
                dve.tensor_copy(wa2_rep[:], wa2[:].to_broadcast([P, P])).then_inc(setup_dve, 1)
                dve.wait_ge(gate_hi, 1)
                dve.scalar_tensor_tensor(gate_l[:], gate_f[:], WSCALE, gate_h[:], ALU.mult,
                                         ALU.subtract).then_inc(setup_dve, 1)

            def stats(i, db, src, st, mv, done):
                for c in range(C):
                    dve.bn_stats(st[:, c, :], src[:, c, :]).then_inc(done, 1)
                for c in range(C):
                    if c == 0:
                        dve.wait_ge(done, count(i, STATS, db, C))
                        dve.memset(carrier[:], 0.0)
                    dve.bn_aggr(mv[:, c, :], st[:, c, :]).then_inc(done, 1)

            def normed(i, db, dst, src, mv, rs, rstd, done):
                dve.wait_ge(rstd, count(i, 2, db, 2))
                for c in range(C):
                    ins = dve.tensor_scalar(dst[:, c, :], src[:, c, :], mv[:, c, 0:1], rs[:, 1, c:c + 1],
                                            ALU.subtract, ALU.mult)
                ins.then_inc(done, 1)

            def softmax_logits(i, db, part):
                def at(n):
                    return count(i, SOFT, db, n)

                if part == 1:
                    dve.wait_ge(a_soft, at(5))
                    dve.scalar_tensor_tensor(s1c[:, 3, :], s1c[:, 2, :], ALPHA, s1c[:, 2, :], ALU.mult, ALU.max)\
                       .then_inc(a_soft, 1)
                    dve.scalar_tensor_tensor(u_a[:], u_a[:], ALPHA, u_a[:], ALU.mult, ALU.max).then_inc(a_soft, 1)
                    dve.wait_ge(a_soft, at(7))
                    dve.tensor_tensor(u_a[:], u_a[:], bcast(s1c[:, 3, :], nodes), ALU.subtract).then_inc(a_soft, 1)
                    return
                dve.wait_ge(a_s1p, count(i, 1, db, 1))
                dve.tensor_reduce(s1c[:, 0, :], s1p[:], AX_X, ALU.add).then_inc(a_soft, 1)
                dve.wait_ge(a_s, count(i, 1, db, 1))
                s2j = s0[:].rearrange("p (c g n) -> p c g n", c=C, g=gpt)
                for h in range(gpt):
                    ps = slice(h * nodes, (h + 1) * nodes)
                    dve.tensor_reduce(s1c[ps, 1, :], s2j[ps, :, h, :], AX_X, ALU.max).then_inc(a_soft, 1)
                dve.wait_ge(a_soft, at(3))
                for h in range(gpt):
                    ps = slice(h * nodes, (h + 1) * nodes)
                    ins = dve.tensor_tensor(u_a[ps], s2j[ps, :, h, :], bcast(s1c[ps, 0, :], nodes), ALU.add)
                ins.then_inc(a_soft, 1)
                dve.tensor_tensor(s1c[:, 2, :], s1c[:, 0, :], s1c[:, 1, :], ALU.add).then_inc(a_soft, 1)

            def softmax_numerators(i, db):
                dve.wait_ge(a_exp, count(i, 1, db, 1))
                dve.wait_ge(adja_landed, count(i, 16, db, 16))
                for h in range(gpt):
                    ps = slice(h * nodes, (h + 1) * nodes)
                    ins = dve.scalar_tensor_tensor(pr_a[ps, :, ps], adj_a[ps], 1.0e-6, e_a[ps], ALU.add, ALU.mult)
                ins.then_inc(a_prob, 1)

            def softmax_sums(i, db):
                dve.wait_ge(a_prob, count(i, 1, db, 1))
                dve.tensor_reduce(row_sum[:], pr_a[:], AX_X, ALU.add).then_inc(a_sum, 1)
                dve.wait_ge(a_sum, count(i, 1, db, 1))
                dve.reciprocal(rr_a[:], row_sum[:]).then_inc(a_x1n, 1)

            def add_attention(i, db):
                dve.wait_ge(a_out, count(i, 1, db, 1))
                dve.wait_ge(a_x1n, count(i, X1N, db, 1))
                for c in range(C):
                    dve.scalar_tensor_tensor(x1n[:, c, :], s0[:, c * D:(c + 1) * D], rr_a[:, c:c + 1], x_in[:, c, :],
                                             ALU.mult, ALU.add).then_inc(a_x1n, 1)

            def low_parts(i, db, g, parts, bank):
                dve.wait_ge(g.hi_s, count(i, 1, db, 1))
                dve.tensor_tensor(parts[:, 1, :], bank[:], parts[:, 0, :], ALU.subtract).then_inc(g.lo_s, 1)

            def xb_low(i, db):
                dve.wait_ge(b_xt, count(i, 1, db, 1))
                dve.tensor_tensor(xt_b[:, 1, :], s1[:], xt_b[:, 0, :], ALU.subtract).then_inc(b_xlo, 1)

            def top_two(i, db, g, bank, part):
                def after(n):
                    dve.wait_ge(g.top, count(i, TOP, db, n))

                def largest(k, src, n):
                    after(n)
                    dve.tensor_reduce(g.m[:, 2 * k, :], src[:], AX_X, ALU.max).then_inc(g.top, 1)

                def equal(k, src, n):
                    after(n)
                    dve.tensor_tensor(g.q[:, 2 * k], src[:], bcast(g.m[:, 2 * k, :], E), ALU.is_equal).then_inc(g.top, 1)

                def ranked(k, n):
                    after(n)
                    dve.tensor_tensor(g.q[:, 2 * k + 1], g.q[:, 2 * k],
                                      ramp[:].unsqueeze(1).to_broadcast([P, C, E]), ALU.mult).then_inc(g.top, 1)

                def first_of_equal(k, n):
                    after(n)
                    dve.tensor_reduce(g.m[:, 2 * k + 1, :], g.q[:, 2 * k + 1], AX_X, ALU.max).then_inc(g.top, 1)
                    after(n + 1)
                    dve.tensor_tensor(g.one[:, k], g.q[:, 2 * k + 1], bcast(g.m[:, 2 * k + 1, :], E), ALU.is_equal)\
                       .then_inc(g.top, 1)

                if part == 0:
                    logits = bank[:, 0:C * E].rearrange("p (c e) -> p c e", c=C)
                    dve.wait_ge(g.logits, count(i, 1, db, 1))
                    if g is gates[0]:
                        dve.tensor_scalar(g.lg[:], logits, 1.0 / WSCALE, None, ALU.mult).then_inc(g.top, 1)
                    else:
                        if isinstance(i, int) and i == 1:
                            dve.wait_ge(layer1_in, 16 * 4)
                        dve.scalar_tensor_tensor(g.lg[:], logits, 1.0 / WSCALE,
                                                 bg_b[:].unsqueeze(1).to_broadcast([P, C, E]), ALU.mult,
                                                 ALU.add).then_inc(g.top, 1)
                    largest(0, g.lg, 1)
                    equal(0, g.lg, 2)
                    ranked(0, 3)
                if part == 1:
                    first_of_equal(0, 4)
                    after(6)
                    dve.scalar_tensor_tensor(g.lg2[:], g.one[:, 0], NOT_AGAIN, g.lg[:], ALU.mult, ALU.add)\
                       .then_inc(g.top, 1)
                    largest(1, g.lg2, 7)
                if part == 2:
                    equal(1, g.lg2, 8)
                    ranked(1, 9)
                    first_of_equal(1, 10)
                    dve.tensor_tensor(g.m[:, 4, :], g.m[:, 2, :], g.m[:, 0, :], ALU.subtract).then_inc(g.top, 1)

            def masks(i, db, g):
                if g is gates[0]:
                    dve.wait_ge(g.tanh, count(i, 1, db, 1))
                    dve.tensor_scalar(g.w[:, 0, :], g.th[:], -0.5, 0.5, ALU.mult, ALU.add).then_inc(g.mask_d, 1)
                    dve.tensor_scalar(g.w[:, 1, :], g.th[:], 0.5, 0.5, ALU.mult, ALU.add).then_inc(g.mask_d, 1)
                    dve.wait_ge(g.mask_d, count(i, 5, db, 2))
                    for k in range(TOPS):
                        dve.tensor_tensor(g.q[:, k], g.one[:, k], bcast(g.w[:, k, :], E), ALU.mult)\
                           .then_inc(g.mask_d, 1)
                    dve.wait_ge(g.mask_d, count(i, 5, db, 4))
                    a, b = g.q[:, 0], g.q[:, 1]
                else:
                    a, b = g.one[:, 0], g.one[:, 1]
                    dve.wait_ge(g.top, count(i, TOP, db, TOP))
                dve.tensor_tensor(g.mask[:].rearrange("p e c -> p c e"), a, b, ALU.add).then_inc(g.mask_d, 1)

            def unit_out(i, u, back=0):
                g = gates[0] if u < A_UNITS else gates[1]
                dve.wait_ge(down, chunks(i, LAST[u] + 1, back))
                y = ps_y[u % 2]
                if u == 0:
                    dve.tensor_scalar(g.acc[:], y[:], b2x[:, 0:1], 1.0 / WSCALE, ALU.add, ALU.mult).then_inc(evac, 1)
                    return
                e = (u - 1) % E
                if e % 2 == 0:
                    dve.wait_ge(g.mb_in[e // 2], count(i, 16, 0 if u < A_UNITS else -1 - back, 16))
                dst = g.acc if u == A_UNITS else scaled
                if dst is scaled:
                    need(dve, summed, sums(i, u, back))
                dve.scalar_tensor_tensor(dst[:], y[:], b2x[:, u:u + 1], g.mb[:, e, :], ALU.add, ALU.mult)\
                   .then_inc(evac, 1)

            def finish(i, db):
                dve.wait_ge(gates[1].acc_tr, count(i, 1, db, 1))
                need(dve, stored, count(i, 16, db, 0))
                dve.tensor_tensor(x4[:], s0[:].rearrange("p (c d) -> p c d", c=C), x3[:], ALU.add)\
                   .then_inc(x4_made, 1)

            def iteration(i):
                experts0, layer1, next0, last1 = has(i)
                for s in range(SLOTS):
                    if isinstance(i, int) and i == -1 and s == SETUP_AT:
                        setup()
                    if layer1:
                        if s == 1 and isinstance(i, int) and i == 1:
                            dve.wait_ge(gcn_hi, 1)
                            dve.scalar_tensor_tensor(gcn_l[:], gcn_f[:], WSCALE, gcn_h[:], ALU.mult,
                                                     ALU.subtract).then_inc(gcn_lo, 1)
                        if s == DVE_AT["f_b"]:
                            dve.wait_ge(b_f, count(i, 1, -1, 1))
                            dve.wait_ge(b_norm, count(i, 2, -1, 2))
                            dve.scalar_tensor_tensor(f_b[:], s1[:].rearrange("p (c d) -> p c d", c=C), 1.0 / WSCALE,
                                                     bcast(dg_b[:, 2, :], D), ALU.mult, ALU.mult).then_inc(b_fn, 1)
                        if s == DVE_AT["mix_1"]:
                            dve.wait_ge(b_hets, count(i, 1, -1, 1))
                            dve.wait_ge(b_hom, count(i, 1, -1, 1))
                            dve.tensor_tensor(d_b[:], s2[:], het_b[:], ALU.subtract).then_inc(b_mix, 1)
                            dve.wait_ge(b_tanh, count(i, 1, -1, 1))
                            dve.wait_ge(b_mix, count(i, MIX, -1, 1))
                            dve.scalar_tensor_tensor(d_b[:], tg_b[:], 1.0, d_b[:], ALU.add, ALU.mult).then_inc(b_mix, 1)
                        if s == DVE_AT["mix_2"]:
                            dve.wait_ge(b_mix, count(i, MIX, -1, 2))
                            dve.scalar_tensor_tensor(o_b[:], d_b[:], 0.5, het_b[:], ALU.mult, ALU.add).then_inc(b_mix, 1)
                        if s == DVE_AT["mix_3"]:
                            dve.wait_ge(b_mix, count(i, MIX, -1, 3))
                            dve.tensor_scalar(d_b[:], o_b[:], 0.0, None, ALU.min).then_inc(b_mix, 1)
                        if s == DVE_AT["elu"]:
                            dve.wait_ge(b_exp, count(i, 1, -1, 1))
                            dve.scalar_tensor_tensor(o_b[:], o_b[:], 0.0, d_b[:], ALU.max, ALU.add).then_inc(b_elu, 1)
                        if s == DVE_AT["x3"]:
                            dve.wait_ge(b_otr, count(i, 1, -1, 1))
                            dve.scalar_tensor_tensor(x3[:], s1[:].rearrange("p (c d) -> p c d", c=C), -1.0, x2[:],
                                                     ALU.add, ALU.add).then_inc(x3_made, 1)
                        if s == DVE_AT["stats_1"]:
                            dve.wait_ge(x3_made, count(i, 1, -1, 1))
                            stats(i, -1, x3, gates[1].st, gates[1].mv, gates[1].stats)
                        if s == DVE_AT["norm_1"]:
                            normed(i, -1, gates[1].xn, x3, gates[1].mv, gates[1].rs, gates[1].rstd, gates[1].xn_s)
                        if s == DVE_AT["low_1"]:
                            low_parts(i, -1, gates[1], gates[1].xt, s1)
                        if s in DVE_AT["top_1"]:
                            top_two(i, -1, gates[1], s2, DVE_AT["top_1"].index(s))
                        if s == DVE_AT["masks_1"]:
                            masks(i, -1, gates[1])
                    if next0:
                        if s == DVE_AT["stats_a"]:
                            dve.wait_ge(x_landed, count(i, 16, 1, 16))
                            stats(i, 1, x_in, st_a, mv_a, a_stats)
                        if s == DVE_AT["norm_a"]:
                            normed(i, 1, xn_a, x_in, mv_a, rs_a, a_rstd, a_xn)
                        if s in DVE_AT["softmax"]:
                            softmax_logits(i, 1, DVE_AT["softmax"].index(s))
                        if s == DVE_AT["numerators"]:
                            softmax_numerators(i, 1)
                        if s == DVE_AT["sums"]:
                            softmax_sums(i, 1)
                        if s == DVE_AT["attend"]:
                            add_attention(i, 1)
                        if s == DVE_AT["stats_0"]:
                            dve.wait_ge(a_x1n, count(i, X1N, 1, X1N))
                            stats(i, 1, x1n, gates[0].st, gates[0].mv, gates[0].stats)
                        if s == DVE_AT["norm_0"]:
                            normed(i, 1, gates[0].xn, x1n, gates[0].mv, gates[0].rs, gates[0].rstd, gates[0].xn_s)
                        if s == DVE_AT["low_0"]:
                            low_parts(i, 1, gates[0], gates[0].next, s0)
                        if s in DVE_AT["top_0"]:
                            top_two(i, 1, gates[0], s1, DVE_AT["top_0"].index(s))
                        if s == DVE_AT["low_0" if is_fill(i) else "move_0"]:
                            dve.wait_ge(gates[0].lo_s, count(i, 1, 1, 1))
                            if experts0:
                                dve.wait_ge(up, chunks(i, A_SLOTS))
                            dve.tensor_copy(gates[0].xt[:], gates[0].next[:]).then_inc(gates[0].moved, 1)
                        if s == DVE_AT["masks_0"] and not is_fill(i):
                            masks(i, 1, gates[0])
                    if is_first(i) and s == MASKS_LATE:
                        masks(i, 0, gates[0])
                    if s == DVE_AT["x2"]:
                        if experts0:
                            dve.wait_ge(gates[0].acc_tr, count(i, 1, 0, 1))
                            dve.tensor_tensor(x2[:], s2[:].rearrange("p (c d) -> p c d", c=C), x1[:], ALU.add)\
                               .then_inc(x2_made, 1)
                            dve.wait_ge(x2_made, count(i, 1, 0, 1))
                            stats(i, 0, x2, st_b, mv_b, b_stats)
                    if s == DVE_AT["x1"]:
                        if experts0:
                            dve.wait_ge(adjb_landed, count(i, 16, 0, 16))
                            dve.tensor_reduce(dg_b[:, 0, :], adj_b[:], AX_X, ALU.add).then_inc(b_deg, 1)
                        if next0:
                            if not experts0:
                                dve.wait_ge(a_x1n, count(i, X1N, 1, X1N))
                            dve.tensor_copy(x1[:], x1n[:]).then_inc(x1_made, 1)
                    if experts0 and s == DVE_AT["low_b"] and not is_first(i):
                        xb_low(i, 0)
                    if s == XB_LATE and isinstance(i, int) and is_first(i - 1):
                        xb_low(i, -1)
                    if experts0 and s == DVE_AT["norm_b"]:
                        normed(i, 0, xn_b, x2, mv_b, rs_b, b_rstd, b_xn)
                    if ((experts0 and s < A_SLOTS) or (layer1 and s >= A_SLOTS)) and s in CAST:
                        dve.wait_ge(gelu, chunks(i, s + 1))
                        dve.tensor_copy(hhi[s % H_SLOTS][:], h32[s % H_SLOTS][:]).then_inc(cast, 1)
                    if ((experts0 and s < A_SLOTS) or (layer1 and s >= A_SLOTS)) and s in BY_DVE:
                        k = s % H_SLOTS
                        if s in CAST:
                            dve.wait_ge(cast, those(i, s + 1, CAST))
                        else:
                            dve.wait_ge(gelu, chunks(i, s + 1))
                        dve.tensor_tensor(hlo[k][:], h32[k][:], hhi[k][:], ALU.subtract).then_inc(low, 1)
                    for u in range(UNITS):
                        if LAST[u] + LAG == s and (experts0 if u < A_UNITS else layer1):
                            unit_out(i, u)
                        if LAST[u] + LAG == s + SLOTS and last1:
                            unit_out(i, u, 1)
                    if last1 and s == DVE_AT["x4"]:
                        finish(i, -2)
                    if isinstance(i, int) and i < 1:
                        for n in range(2 * PIECES):
                            if PIECE_AT[n] == (i + 1) * SLOTS + s:
                                weight_piece(n)
                if isinstance(i, int) and i == NB:
                    for u in range(UNITS):
                        if LAST[u] + LAG >= SLOTS:
                            unit_out(i, u)
                    finish(i, -1)

            in_blocks(dve, iteration)

        @block.tensor
        def _(pe):
            def transposes(bank, src):
                for c in range(C):
                    ins = pe.transpose(bank[:, c * P:(c + 1) * P], src[:, c * P:(c + 1) * P], ident[:])
                return ins

            def flat(t):
                return t[:].rearrange("p c d -> p (c d)")

            def setup():
                pe.wait_ge(consts, CONSTS)
                pe.wait_ge(small_in, 16 * SMALL)
                pe.transpose(s1[:, 0:ROWS], rows[:], ident[0:ROWS, 0:ROWS])
                pe.transpose(s2[:, 0:D], gat_w[:], ident[:]).then_inc(setup_pe, 1)
                pe.wait_ge(setup_dve, 4)
                pe.matmul(s1[:, 0:D], a1_rep[:], gat_wT[:], start=True, stop=True)
                pe.matmul(s2[:, 0:1], gat_wT[:], cols[:, A_ROW + 1:A_ROW + 2], start=True, stop=True)\
                  .then_inc(setup_pe, 1)

            def up_product(i, s):
                g = gates[0] if s < A_SLOTS else gates[1]
                if s == 0:
                    pe.wait_ge(g.moved, count(i, 1, 0, 1))
                if s == A_SLOTS:
                    pe.wait_ge(g.lo_s, count(i, 1, -1, 1))
                if isinstance(i, int) and i <= 1:
                    pe.wait_ge(w_lo, min(2 * (s // C + 1), 2 * PIECES))
                need(pe, gelu, bank_free(i, s))
                h = ps_h[H_BANK[s]]
                pe.matmul(h[:], w1h[:, s, :], g.xt[:, 0, :], start=True, stop=False)
                pe.matmul(h[:], w1l[:, s, :], g.xt[:, 0, :], start=False, stop=False)
                pe.matmul(h[:], w1h[:, s, :], g.xt[:, 1, :], start=False, stop=True).then_inc(up, 1)

            def down_product(i, s, back=0):
                u = UNIT_OF[s]
                k = s % H_SLOTS
                y = ps_y[u % 2]
                first, last = s == FIRST[u], s == LAST[u]
                if first:
                    need(pe, evac, units(i, 0, back) if u == 0 else units(i, u, back) - 1)
                if s in WHOLE:
                    pe.wait_ge(gelu, chunks(i, s + 1, back))
                    pe.matmul(y[:], w2f[:, WHOLE.index(s), :], h32[k][:], start=first, stop=last).then_inc(down, 1)
                    return
                if s in BY_POOL:
                    pe.wait_ge(low_pool, those(i, s + 1, BY_POOL, back))
                else:
                    pe.wait_ge(low, those(i, s + 1, BY_DVE, back))
                pe.matmul(y[:], w2h[:, s, :], hhi[k][:], start=first, stop=False)
                pe.matmul(y[:], w2l[:, s, :], hhi[k][:], start=False, stop=False)
                pe.matmul(y[:], w2h[:, s, :], hlo[k][:], start=False, stop=last).then_inc(down, 1)

            def logits(i, db, g, parts, n, bank):
                pe.wait_ge(g.lo_s, count(i, 1, db, 1))
                for c in range(C):
                    o = bank[:, c * E:(c + 1) * E]
                    t = slice(c * P, (c + 1) * P)
                    pe.matmul(o, parts[:, 0, t], gate_h[:, n, :], start=True, stop=False)
                    pe.matmul(o, parts[:, 0, t], gate_l[:, n, :], start=False, stop=False)
                    ins = pe.matmul(o, parts[:, 1, t], gate_h[:, n, :], start=False, stop=True)
                ins.then_inc(g.logits, 1)

            def mask_transpose(i, db, g, bank):
                pe.wait_ge(g.mask_d, count(i, 5 if g is gates[0] else 1, db, 5 if g is gates[0] else 1))
                pe.transpose(bank[0:E * C, 0:P], g.mask[:].rearrange("p e c -> p (e c)"), ident[:])\
                  .then_inc(g.mask_tr, 1)

            def xb_product(bank, w):
                pe.matmul(bank[:], gcn_h[:, w, :], xt_b[:, 0, :], start=True, stop=False)
                pe.matmul(bank[:], gcn_l[:, w, :], xt_b[:, 0, :], start=False, stop=False)
                return pe.matmul(bank[:], gcn_h[:, w, :], xt_b[:, 1, :], start=False, stop=True)

            def xb_transpose(i, db):
                pe.wait_ge(b_xn, count(i, 1, db, 1))
                if not isinstance(i, int) or i + db + 1 < NB:
                    pe.wait_ge(gates[0].mask_row, count(i, 1, db + 1, 1))
                transposes(s1, flat(xn_b)).then_inc(b_tr, 1)

            def acc_transpose(i, db):
                pe.wait_ge(summed, sums(i, UNITS, -1 - db))
                transposes(s0, gates[1].acc).then_inc(gates[1].acc_tr, 1)

            def iteration(i):
                experts0, layer1, next0, last1 = has(i)
                for s in range(SLOTS):
                    if isinstance(i, int) and i == -1 and s == SETUP_AT:
                        setup()
                    if s == XB_LATE and isinstance(i, int) and is_first(i - 1):
                        xb_transpose(i, -1)
                    if layer1:
                        if s == PE_AT["f"]:
                            if isinstance(i, int) and i == 1:
                                pe.wait_ge(gcn_lo, 1)
                            pe.wait_ge(b_xlo, count(i, 1, -1, 1))
                            for c in range(C):
                                t = slice(c * P, (c + 1) * P)
                                o = s1[:, c * D:(c + 1) * D]
                                pe.matmul(o, xt_b[:, 0, t], gcn_h[:, THETA, :], start=True, stop=False)
                                pe.matmul(o, xt_b[:, 0, t], gcn_l[:, THETA, :], start=False, stop=False)
                                ins = pe.matmul(o, xt_b[:, 1, t], gcn_h[:, THETA, :], start=False, stop=True)
                            ins.then_inc(b_f, 1)
                        if s == PE_AT["adj_tr"]:
                            pe.wait_ge(b_adjn, count(i, 2, -1, 2))
                            transposes(s2, flat(an_b)).then_inc(b_atr, 1)
                        if s == PE_AT["gate_b"]:
                            xb_product(s0, WT).then_inc(b_gate, 1)
                        if s == PE_AT["acc1_tr"] and last1:
                            pe.wait_ge(b_tanh, count(i, 1, -1, 1))
                            acc_transpose(i, -2)
                        if s == PE_AT["het"]:
                            pe.wait_ge(b_fn, count(i, 1, -1, 1))
                            xb_product(s1, WH).then_inc(b_het, 1)
                        if s == PE_AT["hom"]:
                            pe.wait_ge(b_at, count(i, 1, -1, 1))
                            for c in range(C):
                                t = slice(c * P, (c + 1) * P)
                                ins = pe.matmul(s2[:, t], f_b[:, c, :], at_b[:, t], start=True, stop=True)
                            ins.then_inc(b_hom, 1)
                        if s == PE_AT["o_tr"]:
                            pe.wait_ge(b_elu, count(i, 1, -1, 1))
                            transposes(s1, o_b).then_inc(b_otr, 1)
                        if s == PE_AT["xn1_tr"]:
                            pe.wait_ge(gates[1].xn_s, count(i, 1, -1, 1))
                            transposes(s1, flat(gates[1].xn)).then_inc(gates[1].tr, 1)
                        if s == PE_AT["logits_1"]:
                            logits(i, -1, gates[1], gates[1].xt, 1, s2)
                        if s == PE_AT["mask1_tr"]:
                            mask_transpose(i, -1, gates[1], s2)
                    if next0:
                        if s == PE_AT["xa_tr"]:
                            pe.wait_ge(a_xn, count(i, 1, 1, 1))
                            if last1:
                                pe.wait_ge(x4_made, count(i, 1, -2, 1))
                            elif layer1:
                                pe.wait_ge(b_tanh, count(i, 1, -1, 1))
                            if isinstance(i, int) and i == -1:
                                pe.wait_ge(consts, CONSTS)
                            transposes(s0, flat(xn_a)).then_inc(a_tr, 1)
                        if s == PE_AT["scores"]:
                            pe.wait_ge(a_xt, count(i, 1, 1, 1))
                            if isinstance(i, int) and i == -1:
                                pe.wait_ge(setup_dve, 8)
                            pe.matmul(s0[:], wa2_rep[:], xt_a[:], start=True, stop=True).then_inc(a_s, 1)
                        if s == PE_AT["wh"]:
                            if layer1:
                                pe.wait_ge(b_mix, count(i, MIX, -1, 1))
                            for c in range(C):
                                ins = pe.matmul(s2[:, c * D:(c + 1) * D], xt_a[:, c * P:(c + 1) * P], gat_w[:],
                                                start=True, stop=True)
                            ins.then_inc(a_wh, 1)
                        if s == PE_AT["p_tr"]:
                            pe.wait_ge(a_prob, count(i, 1, 1, 1))
                            transposes(s0, flat(pr_a)).then_inc(a_ptr, 1)
                        if s == PE_AT["out"]:
                            pe.wait_ge(a_pt, count(i, 1, 1, 1))
                            pe.wait_ge(a_whs, count(i, 1, 1, 1))
                            for c in range(C):
                                t = slice(c * P, (c + 1) * P)
                                ins = pe.matmul(s0[:, t], pt_a[:, t], wh_a[:, t], start=True, stop=True)
                            ins.then_inc(a_out, 1)
                        if s == PE_AT["xn0_tr"]:
                            pe.wait_ge(gates[0].xn_s, count(i, 1, 1, 1))
                            transposes(s0, flat(gates[0].xn)).then_inc(gates[0].tr, 1)
                        if s == PE_AT["logits_0"]:
                            logits(i, 1, gates[0], gates[0].next, 0, s1)
                        if s == PE_AT["mask0_tr"] and not is_fill(i):
                            mask_transpose(i, 1, gates[0], s1)
                    if is_first(i) and s == MASK_TR_LATE:
                        mask_transpose(i, 0, gates[0], s1)
                    if experts0:
                        if s == PE_AT["acc0_tr"]:
                            pe.wait_ge(summed, sums(i, A_UNITS))
                            if layer1:
                                pe.wait_ge(gates[1].mask_row, count(i, 1, -1, 1))
                            transposes(s2, gates[0].acc).then_inc(gates[0].acc_tr, 1)
                        if s == PE_AT["xb_tr"] and not is_first(i):
                            xb_transpose(i, 0)
                    if (experts0 and s < A_SLOTS) or (layer1 and s >= A_SLOTS):
                        up_product(i, s)
                    t = s - LAG
                    if t >= 0 and ((experts0 and t < A_SLOTS) or (layer1 and t >= A_SLOTS)):
                        down_product(i, t)
                    if t < 0 and last1:
                        down_product(i, t + SLOTS, 1)
                if isinstance(i, int) and i == NB:
                    for t in range(SLOTS - LAG, SLOTS):
                        down_product(i, t)
                    acc_transpose(i, -1)

            in_blocks(pe, iteration)


_NAMES = ["x", "adj", "L0_gnn_W", "L0_gnn_a", "L0_ffn_Wr", "L0_ffn_W1s", "L0_ffn_b1s", "L0_ffn_W2s", "L0_ffn_b2s",
          "L0_ffn_W1p", "L0_ffn_b1p", "L0_ffn_W2p", "L0_ffn_b2p", "L1_gnn_W_t", "L1_gnn_b_t", "L1_gnn_W_h",
          "L1_gnn_theta", "L1_ffn_Wg", "L1_ffn_bg", "L1_ffn_W1", "L1_ffn_b1", "L1_ffn_W2", "L1_ffn_b2"]


def kernel(**inputs):
    import numpy as np
    import concourse.bacc as bacc
    from concourse.bass_utils import run_bass_kernel_spmd

    nc = bacc.Bacc("TRN2", target_bir_lowering=False, num_devices=1)
    arrays, args = {}, []
    for name in _NAMES:
        a = np.ascontiguousarray(inputs[name])
        arrays[f"in_{name}"] = a
        args.append(nc.dram_tensor(f"in_{name}", a.shape, mybir.dt.from_np(a.dtype), kind="ExternalInput").ap())
    args.append(nc.dram_tensor("result", inputs["x"].shape, F32, kind="ExternalOutput").ap())
    mk_adj_ffn_kernel(nc, *args)
    r = run_bass_kernel_spmd(nc, [arrays], core_ids=[0])
    return r.results[0]["result"]
```
